# Optimizing a Trainium2 kernel written in Bass

```python
import numpy as np
import jax
import jax.numpy as jnp

def _softmax(x, axis=-1):
    return jax.nn.softmax(x, axis=axis)

def _gelu(x):
    return jax.nn.gelu(x, approximate=True)

def _silu(x):
    return jax.nn.silu(x)

def _sigmoid(x):
    return jax.nn.sigmoid(x)

def _layernorm(x, axis=-1, eps=1e-05):
    m = jnp.mean(x, axis=axis, keepdims=True)
    v = jnp.var(x, axis=axis, keepdims=True)
    return (x - m) / jnp.sqrt(v + eps)

def _scatter_add(tgt, idx, src, axis=0):
    return tgt.at[idx].add(src)

def _segment_sum(src, seg, n):
    return jax.ops.segment_sum(src, seg, n)
kernel_name = 'mk_adaln_ffn_d1_seqx_r8_5b58a1'

def setup_inputs(seed: int=0):
    np.random.seed(seed)
    _w = jnp.asarray

    def _rec_inputs():
        import jax
        import jax.numpy as jnp
        _rk = jax.random.key(seed)
        x = -0.0002928 + 1 * jax.random.normal(jax.random.fold_in(_rk, 1), (32, 128, 128), jnp.float32)
        _lenS = 128 - jax.random.randint(jax.random.fold_in(_rk, 7), (32,), 0, max(1, 128 // 4) + 1, jnp.int32)
        _lenS2 = 128 - jax.random.randint(jax.random.fold_in(_rk, 8), (32,), 0, max(1, 128 // 4) + 1, jnp.int32)
        fside_BxS_0 = 0.0061147 + 1.02565 * jax.random.normal(jax.random.fold_in(_rk, 12), (32, 128), jnp.float32)
        itok_BxSxS_0_4 = jax.random.randint(jax.random.fold_in(_rk, 13), (32, 128, 128), 0, 5, jnp.int32)
        fside_BxSxS_0 = -3.24666e-05 + 0.0312493 * jax.random.normal(jax.random.fold_in(_rk, 14), (32, 128, 128), jnp.float32)
        cond_2048 = -4.62462e-05 + 0.0441849 * jax.random.normal(jax.random.fold_in(_rk, 16), (32, 256), jnp.float32)
        _validS = jnp.arange(128)[None, :] < _lenS[:, None]
        _validS2 = jnp.arange(128)[None, :] < _lenS2[:, None]
        _causal = jnp.tril(jnp.ones((128, 128), dtype=bool))
        mask_BxS_ff1 = jnp.where(jnp.ones((32, 128), dtype=bool), 1.0, 0.0).astype(jnp.float32)
        mask_BxS_ff0 = jnp.where(jnp.ones((32, 128), dtype=bool), 0.0, -1000000000.0).astype(jnp.float32)
        return (x, fside_BxS_0, itok_BxSxS_0_4, fside_BxSxS_0, cond_2048, mask_BxS_ff1, mask_BxS_ff0)
    x, fside_BxS_0, itok_BxSxS_0_4, fside_BxSxS_0, cond_2048, mask_BxS_ff1, mask_BxS_ff0 = _rec_inputs()

    def _L0_cond_setup():
        import jax, jax.numpy as jnp
        import numpy as np
        B, N, D = (4, 128, 128)
        T_ITER = 4
        E_TYPES = 4
        ALPHA = 0.2

        def _lin_w(key, out_f, in_f):
            bound = float(np.sqrt(3.0 / ((in_f + out_f) / 2.0)))
            return jax.random.uniform(key, (out_f, in_f), minval=-bound, maxval=bound, dtype=jnp.float32)

        def _lin(x, w, b):
            return x @ w.T + b

        def _qdgat_forward(ents, ent_mask, q_encoding, adj, types, init_mem, w_qin, b_qin, w_qt, b_qt, w_pl, b_pl, w_pc, b_pc, w_q, b_q, w_k, b_k, w_v, b_v, w_pk, b_pk, w_pv, b_pv, wes, w_mu, b_mu, w_cb, b_cb):
            d = ents.shape[-1]
            x_loc = ents
            x_ctx = jnp.broadcast_to(init_mem, ents.shape)
            var_drop = ent_mask[:, :, None]
            adj_pos = adj > 0
            q_base = jax.nn.elu(_lin(q_encoding, w_qin, b_qin))
            n_types = wes.shape[0] + 1
            for t in range(T_ITER):
                cmd = _lin(q_base, w_qt[t], b_qt[t])
                xc = x_ctx * var_drop
                pl = _lin(x_loc, w_pl, b_pl)
                pc = _lin(xc, w_pc, b_pc)
                x_joint = jnp.concatenate([x_loc, xc, pl * pc], axis=-1)
                q = _lin(x_joint, w_q, b_q)
                k = _lin(x_joint, w_k, b_k) * _lin(cmd, w_pk, b_pk)[:, None, :]
                v = _lin(x_joint, w_v, b_v) * _lin(cmd, w_pv, b_pv)[:, None, :]
                edge_score = jnp.zeros(adj.shape, jnp.float32)
                for i in range(n_types):
                    if types >> i & 1 == 1:
                        w1, w2 = (wes[i - 1, :d], wes[i - 1, d:])
                        s = (q @ w1)[:, :, None] + (k @ w2)[:, None, :]
                        edge_score = edge_score + jnp.where(adj == i, s, 0.0)
                e = jnp.where(edge_score > 0, edge_score, ALPHA * edge_score)
                logits = jnp.where(adj_pos, e, jnp.float32(-9000000000000000.0))
                prob = jax.nn.softmax(logits, axis=-1)
                message = jnp.einsum('bij,bjd->bid', prob, v)
                x_ctx = _lin(jnp.concatenate([xc, message], axis=-1), w_mu, b_mu)
            return _lin(jnp.concatenate([x_loc, x_ctx], axis=-1), w_cb, b_cb)
        key = jax.random.key(seed)
        ks = jax.random.split(key, 32)
        inp = {}
        inp['ents'] = jax.random.normal(ks[0], (B, N, D), jnp.float32)
        inp['ent_mask'] = jnp.ones((B, N), jnp.float32)
        inp['q_encoding'] = jax.random.normal(ks[1], (B, D), jnp.float32)
        inp['adj'] = jax.random.randint(ks[2], (B, N, N), 0, E_TYPES + 1, dtype=jnp.int32)
        inp['types'] = 30
        inp['init_mem'] = jax.random.normal(ks[3], (1, D), jnp.float32)
        inp['w_qin'] = _lin_w(ks[4], D, D)
        inp['b_qin'] = jnp.zeros((D,), jnp.float32)
        inp['w_qt'] = jnp.stack([_lin_w(ks[5 + t], D, D) for t in range(T_ITER)])
        inp['b_qt'] = jnp.zeros((T_ITER, D), jnp.float32)
        inp['w_pl'] = _lin_w(ks[9], D, D)
        inp['b_pl'] = jnp.zeros((D,), jnp.float32)
        inp['w_pc'] = _lin_w(ks[10], D, D)
        inp['b_pc'] = jnp.zeros((D,), jnp.float32)
        inp['w_q'] = _lin_w(ks[11], D, 3 * D)
        inp['b_q'] = jnp.zeros((D,), jnp.float32)
        inp['w_k'] = _lin_w(ks[12], D, 3 * D)
        inp['b_k'] = jnp.zeros((D,), jnp.float32)
        inp['w_v'] = _lin_w(ks[13], D, 3 * D)
        inp['b_v'] = jnp.zeros((D,), jnp.float32)
        inp['w_pk'] = _lin_w(ks[14], D, D)
        inp['b_pk'] = jnp.zeros((D,), jnp.float32)
        inp['w_pv'] = _lin_w(ks[15], D, D)
        inp['b_pv'] = jnp.zeros((D,), jnp.float32)
        wb = 1.414 * float(np.sqrt(6.0 / (2 * D + 1)))
        inp['wes'] = jax.random.uniform(ks[16], (E_TYPES, 2 * D), minval=-wb, maxval=wb, dtype=jnp.float32)
        inp['w_mu'] = _lin_w(ks[17], D, 2 * D)
        inp['b_mu'] = jnp.zeros((D,), jnp.float32)
        inp['w_cb'] = _lin_w(ks[18], D, 2 * D)
        inp['b_cb'] = jnp.zeros((D,), jnp.float32)
        return inp
    _L0_cond_all = _L0_cond_setup()
    _L0_cond_in = {k: v for k, v in _L0_cond_all.items() if k in ('init_mem', 'w_qin', 'b_qin', 'w_pl', 'b_pl', 'w_pc', 'b_pc', 'w_q', 'b_q', 'w_k', 'b_k', 'w_v', 'b_v', 'w_pk', 'b_pk', 'w_pv', 'b_pv', 'w_mu', 'b_mu', 'w_cb', 'b_cb')}
    del _L0_cond_all

    def _L0_ffn_setup():
        import jax, jax.numpy as jnp
        import numpy as np
        TEMPERATURE = 1.0
        TOPK = 2
        key = jax.random.key(seed)
        ks = jax.random.split(key, 6)
        S, B, H, F, E = (256, 4, 128, 512, 8)
        x = jax.random.normal(ks[0], (S, B, H), dtype=jnp.float32)
        gate_w = jax.random.normal(ks[1], (E, H), dtype=jnp.float32) * (1.0 / np.sqrt(H))
        w1 = jax.random.normal(ks[2], (E, H, F), dtype=jnp.float32) * (1.0 / np.sqrt(H))
        b1 = jnp.zeros((E, F), dtype=jnp.float32)
        w2 = jax.random.normal(ks[3], (E, F, H), dtype=jnp.float32) * (1.0 / np.sqrt(F))
        b2 = jnp.zeros((E, H), dtype=jnp.float32)
        return {'x': x, 'gate_w': gate_w, 'w1': w1, 'b1': b1, 'w2': w2, 'b2': b2}
    _L0_ffn_all = _L0_ffn_setup()
    _L0_ffn_in = {k: v for k, v in _L0_ffn_all.items() if k in ('gate_w', 'w1', 'b1', 'w2', 'b2')}
    del _L0_ffn_all
    return {'x': x, 'fside_BxS_0': fside_BxS_0, 'itok_BxSxS_0_4': itok_BxSxS_0_4, 'fside_BxSxS_0': fside_BxSxS_0, 'cond_2048': cond_2048, 'mask_BxS_ff1': mask_BxS_ff1, 'mask_BxS_ff0': mask_BxS_ff0, 'L0_cond_init_mem': _L0_cond_in['init_mem'], 'L0_cond_w_qin': _L0_cond_in['w_qin'], 'L0_cond_b_qin': _L0_cond_in['b_qin'], 'L0_cond_w_pl': _L0_cond_in['w_pl'], 'L0_cond_b_pl': _L0_cond_in['b_pl'], 'L0_cond_w_pc': _L0_cond_in['w_pc'], 'L0_cond_b_pc': _L0_cond_in['b_pc'], 'L0_cond_w_q': _L0_cond_in['w_q'], 'L0_cond_b_q': _L0_cond_in['b_q'], 'L0_cond_w_k': _L0_cond_in['w_k'], 'L0_cond_b_k': _L0_cond_in['b_k'], 'L0_cond_w_v': _L0_cond_in['w_v'], 'L0_cond_b_v': _L0_cond_in['b_v'], 'L0_cond_w_pk': _L0_cond_in['w_pk'], 'L0_cond_b_pk': _L0_cond_in['b_pk'], 'L0_cond_w_pv': _L0_cond_in['w_pv'], 'L0_cond_b_pv': _L0_cond_in['b_pv'], 'L0_cond_w_mu': _L0_cond_in['w_mu'], 'L0_cond_b_mu': _L0_cond_in['b_mu'], 'L0_cond_w_cb': _L0_cond_in['w_cb'], 'L0_cond_b_cb': _L0_cond_in['b_cb'], 'L0_ffn_gate_w': _L0_ffn_in['gate_w'], 'L0_ffn_w1': _L0_ffn_in['w1'], 'L0_ffn_b1': _L0_ffn_in['b1'], 'L0_ffn_w2': _L0_ffn_in['w2'], 'L0_ffn_b2': _L0_ffn_in['b2']}

def reference(x, fside_BxS_0, itok_BxSxS_0_4, fside_BxSxS_0, cond_2048, mask_BxS_ff1, mask_BxS_ff0, L0_cond_init_mem, L0_cond_w_qin, L0_cond_b_qin, L0_cond_w_pl, L0_cond_b_pl, L0_cond_w_pc, L0_cond_b_pc, L0_cond_w_q, L0_cond_b_q, L0_cond_w_k, L0_cond_b_k, L0_cond_w_v, L0_cond_b_v, L0_cond_w_pk, L0_cond_b_pk, L0_cond_w_pv, L0_cond_b_pv, L0_cond_w_mu, L0_cond_b_mu, L0_cond_w_cb, L0_cond_b_cb, L0_ffn_gate_w, L0_ffn_w1, L0_ffn_b1, L0_ffn_w2, L0_ffn_b2):
    import jax
    import jax.numpy as jnp

    def _L0_cond_ref(ents, ent_mask, q_encoding, adj, types, init_mem, w_qin, b_qin, w_qt, b_qt, w_pl, b_pl, w_pc, b_pc, w_q, b_q, w_k, b_k, w_v, b_v, w_pk, b_pk, w_pv, b_pv, wes, w_mu, b_mu, w_cb, b_cb):
        import jax, jax.numpy as jnp
        import numpy as np
        B, N, D = (4, 128, 128)
        T_ITER = 4
        E_TYPES = 4
        ALPHA = 0.2

        def _lin_w(key, out_f, in_f):
            bound = float(np.sqrt(3.0 / ((in_f + out_f) / 2.0)))
            return jax.random.uniform(key, (out_f, in_f), minval=-bound, maxval=bound, dtype=jnp.float32)

        def _lin(x, w, b):
            return x @ w.T + b

        def _qdgat_forward(ents, ent_mask, q_encoding, adj, types, init_mem, w_qin, b_qin, w_qt, b_qt, w_pl, b_pl, w_pc, b_pc, w_q, b_q, w_k, b_k, w_v, b_v, w_pk, b_pk, w_pv, b_pv, wes, w_mu, b_mu, w_cb, b_cb):
            d = ents.shape[-1]
            x_loc = ents
            x_ctx = jnp.broadcast_to(init_mem, ents.shape)
            var_drop = ent_mask[:, :, None]
            adj_pos = adj > 0
            q_base = jax.nn.elu(_lin(q_encoding, w_qin, b_qin))
            n_types = wes.shape[0] + 1
            for t in range(T_ITER):
                cmd = _lin(q_base, w_qt[t], b_qt[t])
                xc = x_ctx * var_drop
                pl = _lin(x_loc, w_pl, b_pl)
                pc = _lin(xc, w_pc, b_pc)
                x_joint = jnp.concatenate([x_loc, xc, pl * pc], axis=-1)
                q = _lin(x_joint, w_q, b_q)
                k = _lin(x_joint, w_k, b_k) * _lin(cmd, w_pk, b_pk)[:, None, :]
                v = _lin(x_joint, w_v, b_v) * _lin(cmd, w_pv, b_pv)[:, None, :]
                edge_score = jnp.zeros(adj.shape, jnp.float32)
                for i in range(n_types):
                    if types >> i & 1 == 1:
                        w1, w2 = (wes[i - 1, :d], wes[i - 1, d:])
                        s = (q @ w1)[:, :, None] + (k @ w2)[:, None, :]
                        edge_score = edge_score + jnp.where(adj == i, s, 0.0)
                e = jnp.where(edge_score > 0, edge_score, ALPHA * edge_score)
                logits = jnp.where(adj_pos, e, jnp.float32(-9000000000000000.0))
                prob = jax.nn.softmax(logits, axis=-1)
                message = jnp.einsum('bij,bjd->bid', prob, v)
                x_ctx = _lin(jnp.concatenate([xc, message], axis=-1), w_mu, b_mu)
            return _lin(jnp.concatenate([x_loc, x_ctx], axis=-1), w_cb, b_cb)
        return _qdgat_forward(ents, ent_mask, q_encoding, adj, types, init_mem, w_qin, b_qin, w_qt, b_qt, w_pl, b_pl, w_pc, b_pc, w_q, b_q, w_k, b_k, w_v, b_v, w_pk, b_pk, w_pv, b_pv, wes, w_mu, b_mu, w_cb, b_cb)

    def _L0_ffn_ref(x, gate_w, w1, b1, w2, b2):
        import jax, jax.numpy as jnp
        import numpy as np
        TEMPERATURE = 1.0
        TOPK = 2
        s, b, h = x.shape
        x_flat = x.reshape(s * b, h)
        logits = x_flat @ gate_w.T
        probs = jax.nn.softmax(logits / TEMPERATURE, axis=-1)
        topk_probs, topk_idx = jax.lax.top_k(probs, TOPK)
        hidden = jax.nn.relu(jnp.einsum('th,ehf->tef', x_flat, w1) + b1[None])
        all_out = jnp.einsum('tef,efh->teh', hidden, w2) + b2[None]
        gathered = jnp.take_along_axis(all_out, topk_idx[:, :, None], axis=1)
        y_flat = jnp.sum(gathered * topk_probs[:, :, None], axis=1)
        return y_flat.reshape(s, b, h)
    x = x + _L0_ffn_ref(_L0_cond_ref(x, mask_BxS_ff1, fside_BxS_0, itok_BxSxS_0_4, 30, L0_cond_init_mem, L0_cond_w_qin, L0_cond_b_qin, fside_BxSxS_0, mask_BxS_ff0, L0_cond_w_pl, L0_cond_b_pl, L0_cond_w_pc, L0_cond_b_pc, L0_cond_w_q, L0_cond_b_q, L0_cond_w_k, L0_cond_b_k, L0_cond_w_v, L0_cond_b_v, L0_cond_w_pk, L0_cond_b_pk, L0_cond_w_pv, L0_cond_b_pv, cond_2048, L0_cond_w_mu, L0_cond_b_mu, L0_cond_w_cb, L0_cond_b_cb), L0_ffn_gate_w, L0_ffn_w1, L0_ffn_b1, L0_ffn_w2, L0_ffn_b2)
    return x

_drawn_inputs = setup_inputs


def setup_inputs(seed=0):
    import zlib

    import numpy as np

    out = dict(_drawn_inputs(seed))
    spreads = {'L0_cond_b_qin': (0.0, 0.363),
     'L0_cond_b_pl': (0.0, 0.331),
     'L0_cond_b_pc': (0.0, 0.8),
     'L0_cond_b_q': (0.0, 0.8),
     'L0_cond_b_k': (0.0, 0.8),
     'L0_cond_b_v': (0.0, 0.1),
     'L0_cond_b_pk': (0.0, 0.8),
     'L0_cond_b_pv': (0.0, 0.1),
     'L0_cond_b_mu': (0.0, 0.1),
     'L0_cond_b_cb': (0.0, 0.1),
     'L0_ffn_b1': (0.0, 0.294),
     'L0_ffn_b2': (0.0, 0.1)}
    factors = {'cond_2048': 4.334,
     'L0_cond_w_pl': 2.695,
     'L0_cond_w_q': 4.399,
     'L0_cond_w_k': 5.81,
     'L0_cond_w_pk': 6.532}
    for name, (base, spread) in spreads.items():
        noise = np.random.default_rng([zlib.crc32(name.encode()), seed]).standard_normal(out[name].shape)
        drawn = base * np.exp(spread * noise) if base else spread * noise
        out[name] = jnp.asarray(drawn.astype(out[name].dtype))
    for name, factor in factors.items():
        out[name] = (out[name] * factor).astype(out[name].dtype)
    return out
```

```python
import concourse.bass as bass
from concourse import mybir
from contextlib import ExitStack

B, N, D = 32, 128, 128
TOK = B * N
STEPS = 4
TYPES = 4
E, F = 8, 512
FC = F // 128
SG = 4
SETS = 2
PAIRS = B // (SG * SETS)
ST = SG * N
NT = TOK // 128
ALPHA = 0.2
BIG = 9000000000000000.0
AC = 2 * TYPES
VW = D + AC

WNAMES = (["qinT"] + [f"qtT{t}" for t in range(STEPS)] + ["pkT", "pvT"] + ["k0", "k1", "k2", "q0", "q1", "q2"]
          + ["plT", "pcT", "v0T", "v1T", "v2T", "mu0T", "mu1T", "cb0T", "cb1T"])
WOFF = {w: D * i for i, w in enumerate(WNAMES)}
TAIL = D * len(WNAMES)
SMALL = [("gateT", E), ("w1T", TYPES), ("w2T", TYPES), ("b_qt", STEPS)] + [
    (b, 1) for b in ("b_qin", "b_pl", "b_pc", "b_q", "b_k", "b_pk", "b_pv", "b_mu", "b_cb", "init")]
for _n, _w in SMALL:
    WOFF[_n] = TAIL
    TAIL += _w
WCOLS = TAIL


def build(nc, xT, x, mask, adj, fsT, wpack, bvrow, w1, b1T, w2, b2, ident_d, bf_d, out):
    fp32, bf16, i32 = mybir.dt.float32, mybir.dt.bfloat16, mybir.dt.int32
    ALU = mybir.AluOpType
    ACT = mybir.ActivationFunctionType
    AX = mybir.AxisListType
    TB = STEPS * B

    ctx = ExitStack()
    with ctx:
        def sb(name, shape, dt=fp32):
            return ctx.enter_context(nc.sbuf_tensor(name, shape, dt))

        def sem(name):
            return ctx.enter_context(nc.semaphore(name))

        def sem2(name):
            return [sem(f"{name}_{s}") for s in range(SETS)]

        W = sb("W", [128, WCOLS])

        def w(name, width=D):
            return W[:, WOFF[name]:WOFF[name] + width]

        bv = sb("bv", [128, D])
        idr = sb("idr", [128, 128 + E])
        ident = idr[:, 0:128]
        rank = idr[:, 128:]
        BFC = 256 + SG * TYPES * 128 * 2
        bfc = sb("bfc", [128, BFC], bf16)
        identb = bfc[:, 0:128]
        negid = bfc[:, 128:256]
        selA = bfc[:, 256:256 + SG * TYPES * 128].rearrange("p (b c) -> p b c", b=SG)
        selC = bfc[:, 256 + SG * TYPES * 128:].rearrange("p (b r i) -> p b r i", b=SG, r=TYPES)
        Q = sb("Q", [128, 3, TYPES])
        fs = sb("fs", [128, B])
        qb_e = sb("qb_e", [128, B])
        qb_r = sb("qb_r", [128, B])
        qbase = sb("qbase", [128, B])
        cmd = sb("cmd", [128, TB])
        ck = sb("ck", [128, TB])
        cv = sb("cv", [128, TB])
        KW = sb("KW", [128, TB, TYPES])
        Kef = sb("Kef", [128, 3, B, STEPS * TYPES])
        bcst = sb("bcst", [128, TYPES + B * STEPS * TYPES])
        xs = [sb(f"xs{s}", [128, ST]) for s in range(SETS)]
        mk = [sb(f"mk{s}", [128, ST]) for s in range(SETS)]
        ad = [sb(f"ad{s}", [128, SG, N], i32) for s in range(SETS)]
        eqn = [sb(f"eqn{s}", [128, SG, TYPES, N], bf16) for s in range(SETS)]
        pl = [sb(f"pl{s}", [128, ST]) for s in range(SETS)]
        xc = [sb(f"xc{s}", [128, ST]) for s in range(SETS)]
        xctx = [sb(f"xctx{s}", [128, ST]) for s in range(SETS)]
        prod = [sb(f"prod{s}", [128, ST]) for s in range(SETS)]
        wx = [sb(f"wx{s}", [128, SG, 2, VW]) for s in range(SETS)]
        loc = [sb(f"loc{s}", [128, SG, VW]) for s in range(SETS)]
        locC = [sb(f"locC{s}", [128, SG, STEPS, TYPES]) for s in range(SETS)]
        vac = [sb(f"vac{s}", [128, SG, VW]) for s in range(SETS)]
        rest = [sb(f"rest{s}", [128, SG, AC]) for s in range(SETS)]
        parts = [sb(f"parts{s}", [128, SG, 32], bf16) for s in range(SETS)]
        acT = [sb(f"acT{s}", [128, 128], bf16) for s in range(SETS)]
        sc = [sb(f"sc{s}", [128, SG, N]) for s in range(SETS)]
        lk = [sb(f"lk{s}", [128, SG, N]) for s in range(SETS)]
        nm = [sb(f"nm{s}", [128, SG]) for s in range(SETS)]
        rs = [sb(f"rs{s}", [128, SG]) for s in range(SETS)]
        ri = [sb(f"ri{s}", [128, SG]) for s in range(SETS)]
        pr = [sb(f"pr{s}", [128, SG, N]) for s in range(SETS)]
        pn = [sb(f"pn{s}", [128, SG, N]) for s in range(SETS)]
        pT = [sb(f"pT{s}", [128, SG, N]) for s in range(SETS)]
        msg = [sb(f"msg{s}", [128, SG, N]) for s in range(SETS)]
        xm = [sb(f"xm{s}", [128, ST]) for s in range(SETS)]
        xmall = sb("xmall", [128, TOK])
        lg = sb("lg", [128, NT, E])
        g1 = sb("g1", [128, NT, E])
        g2 = sb("g2", [128, NT, E])
        g3 = sb("g3", [128, NT, E])
        gsel = sb("gsel", [128, NT, E])
        gates = sb("gates", [128, NT, E])
        gm = sb("gm", [128, NT])
        w1s = sb("w1s", [128, E, F])
        w2s = sb("w2s", [128, E, FC, D])
        b1s = sb("b1s", [128, E * FC])
        b2s = sb("b2s", [E, D])

        PS = [ctx.enter_context(nc.psum_tensor(f"ps{i}", [128, 512], fp32)) for i in range(8)]
        ps_pc, ps_v, ps_mu, ps_s, ps_pt, ps_msg = PS[0], PS[1:3], PS[3], PS[4:6], PS[6], PS[7]
        ps_act = PS[3][:, :].bitcast(bf16)[:, 0:128]

        s_w = sem("weights_loaded")
        s_fw = sem("expert_weights_loaded")
        s_pp = sem("setup_product")
        s_pe_ = sem("setup_scalar_done")
        s_pv_ = sem("setup_vector_done")
        s_x = sem2("set_loaded")
        s_pl = sem2("local_projection")
        s_plr = sem2("local_projection_ready")
        s_lp = sem2("local_product")
        s_lr = sem2("local_ready")
        s_eq = sem2("edge_masks_ready")
        s_xc = sem2("context_ready")
        s_pc = sem2("pc_product")
        s_prod = sem2("gated_product_ready")
        s_wx = sem2("value_weights_ready")
        s_vp = sem2("value_product")
        s_vac = sem2("value_ready")
        s_q = sem("query_base_steps")
        s_cvr = sem("value_command_ready")
        s_st = sem2("score_split_steps")
        s_le = sem2("leaky_done")
        s_ri = sem2("row_sum_inverse")
        s_bp = sem("prep_bank")
        s_spl = sem2("score_parts_ready")
        s_ap = sem2("score_transposed")
        s_at = sem2("score_rows_ready")
        s_s = sem2("edge_scores")
        s_sm = sem2("edge_scores_read")
        s_lk = sem2("logits_ready")
        s_ex = sem2("exp_done")
        s_pn = sem2("probs_ready")
        s_ptp = sem2("probs_transposed")
        s_pt = sem2("probs_T_ready")
        s_mp = sem2("message_product")
        s_mg = sem2("message_ready")
        s_mu = sem2("update_product")
        s_xx = sem2("update_read")
        s_cb = sem2("combined_product")
        s_xm = sem2("combined_ready")
        s_gp = sem2("gate_product")
        s_lg = sem2("gate_logits_ready")
        s_exg = sem("gate_exp_done")
        s_gx = sem("gate_max_subtracted")
        s_ga = sem("gates_ready")

        T = STEPS

        TT = TOK // ST
        gcur = sb("gcur", [128, SG, E])
        gT = sb("gT", [E, ST])
        hT = [sb(f"hT{i}", [128, FC, ST]) for i in range(2)]
        acc = [sb("acc", [128, SG, D])]
        xres = sb("xres", [128, SG, D])
        s_xa = sem("expert_input_ready")
        s_gwork = sem("gate_steps")
        s_gc = sem("gates_copied")
        s_gtp = sem("gates_transposed")
        s_gt = sem("gates_T_ready")
        s_b2 = sem("bias_product")
        s_hp = [sem(f"hidden_product_{c}") for c in range(FC)]
        s_h = [sem(f"hidden_ready_{c}") for c in range(FC)]
        s_yp = sem("expert_product")
        s_acc = sem("expert_added")
        s_acc0 = sem("accumulator_ready")
        s_xr = sem("residual_loaded")
        s_out = sem("stored")
        GATE_OPS = 17

        block = ctx.enter_context(nc.Block())

        from_one = [s_cb, s_xc, s_eq, s_xm, s_lg, s_prod, s_vac, s_xx, s_sm, s_pt, s_mg, s_vp, s_wx, s_xa, s_acc0, s_h, s_acc, s_yp, s_gtp, s_out]

        @block.sync
        def _(sp):
            for group in from_one:
                for one in group if isinstance(group, list) else [group]:
                    sp.sem_inc(one, 1)
            for dst, src in ((W[:, :], wpack), (fs[:, :], fsT), (bv[:, :], bvrow.partition_broadcast(128)), (idr[:, :], ident_d),
                             (bfc[:, :], bf_d)):
                sp.dma_start(dst, src).then_inc(s_w, 16)
            with sp.Fori(0, PAIRS) as p:
                reads = sp.snap(p * (T + 1) + 1)
                edges = sp.snap(p * TYPES + 1)
                tok = [sp.snap((p * SETS + s) * ST) for s in range(SETS)]
                g = [sp.snap((p * SETS + s) * SG) for s in range(SETS)]
                for s in range(SETS):
                    sp.wait_ge(s_cb[s], p + 1)
                    sp.dma_start(xs[s][:, :], xT[:, bass.ds(tok[s], ST)]).then_inc(s_x[s], 16)
                    sp.wait_ge(s_xc[s], reads)
                    sp.dma_start(mk[s][:, :], mask[bass.ds(tok[s], ST)].partition_broadcast(128)).then_inc(s_x[s], 16)
                    sp.wait_ge(s_eq[s], edges)
                    sp.dma_start(ad[s][:, :, :], adj[bass.ds(g[s], SG), :, :].rearrange("g i j -> i g j")).then_inc(s_x[s], 16)
            for dst, src in ((w1s[:, :, :], w1), (w2s[:, :, :, :], w2), (b1s[:, :], b1T), (b2s[:, :], b2)):
                sp.dma_start(dst, src).then_inc(s_fw, 16)
            x_t = x.rearrange("(q g) n d -> q n g d", g=SG)
            out_t = out.rearrange("(q g) n d -> q n g d", g=SG)
            with sp.Fori(0, TT) as q:
                added = sp.snap((q + 1) * E * SG + 1)
                sp.wait_ge(s_acc0, q + 1)
                sp.dma_start(xres[:, :, :], x_t[bass.ds(q, 1), :, :, :].rearrange("q n g d -> (q n) g d")).then_inc(s_xr, 16)
                sp.wait_ge(s_acc, added)
                sp.dma_start(out_t[bass.ds(q, 1), :, :, :].rearrange("q n g d -> (q n) g d"), acc[0][:, :, :]).then_inc(s_out, 16)
            sp.wait_ge(s_out, 16 * TT + 1)

        @block.tensor
        def _(pe):
            def mm(o, l, r, start=True, stop=True, **k):
                return nc.tensor.matmul(o, l, r, start=start, stop=stop, **k)

            pe.wait_ge(s_w, 80)
            mm(PS[0][:, 0:B], w("qinT"), fs[:, :]).then_inc(s_pp, 1)
            pe.wait_ge(s_pv_, 1)
            for t in range(T):
                last = mm(PS[1][:, t * B:(t + 1) * B], w(f"qtT{t}"), qbase[:, :])
            last.then_inc(s_pp, 1)
            pe.wait_ge(s_pe_, 2)
            mm(PS[2][:, 0:TB], w("pkT"), cmd[:, :])
            mm(PS[2][:, TB:2 * TB], w("pvT"), cmd[:, :]).then_inc(s_pp, 1)
            pe.wait_ge(s_pv_, 2)
            kw = KW[:, :, :].rearrange("p a i -> p (a i)")
            for c in range(3):
                mm(PS[3 + c][:, :], w(f"k{c}"), kw)
            for c in range(3):
                mm(PS[6][:, c * TYPES:(c + 1) * TYPES], w(f"q{c}"), w("w1T", TYPES))
            mm(PS[6][:, 16:16 + TYPES], w("b_q", 1).to_broadcast([128, 128]), w("w1T", TYPES))
            mm(PS[7][:, :], w("b_k", 1).to_broadcast([128, 128]), kw).then_inc(s_pp, 1)
            pe.wait_ge(s_pv_, 3)

            with pe.Fori(0, PAIRS) as p:
                for s in range(SETS):
                    pe.wait_ge(s_x[s], 48 * (p + 1))
                    if s:
                        pe.wait_ge(s_plr[0], p + 1)
                        pe.wait_ge(s_lr[0], 2 * (p + 1))
                    else:
                        pe.wait_ge(s_xm[1], p + 1)
                        pe.wait_ge(s_lg[1], p + 1)
                    mm(ps_pc[:, :], w("plT"), xs[s][:, :]).then_inc(s_pl[s], 1)
                    for h in range(2):
                        for g in range(2):
                            b = 2 * h + g
                            o = ps_v[h][:, g * 256:g * 256 + D + TYPES * (1 + T)]
                            xb = xs[s][:, b * N:(b + 1) * N]
                            mm(o[:, 0:D], xb, w("v0T"), stop=False, skip_group_check=True)
                            mm(o[:, D:D + TYPES], xb, Q[:, 0, :], start=False, stop=False, skip_group_check=True)
                            last = mm(o[:, D + TYPES:], xb,
                                      Kef[:, 0, bass.ds((p * SETS + s) * SG + b, 1), :].rearrange("p b c -> p (b c)"),
                                      start=False, skip_group_check=True)
                        last.then_inc(s_lp[s], 1)
                with pe.Fori(0, T) as t:
                    n = p * T + t
                    for s in range(SETS):
                        pe.wait_ge(s_xc[s], p * (T + 1) + t + 2)
                        if s:
                            pe.wait_ge(s_prod[0], n + 2)
                        else:
                            pe.wait_ge(s_prod[1], n + 1)
                            pe.wait_ge(s_plr[1], p + 1)
                        mm(ps_pc[:, :], w("pcT"), xc[s][:, :]).then_inc(s_pc[s], 1)
                    for s in range(SETS):
                        pe.wait_ge(s_prod[s], n + 2)
                        pe.wait_ge(s_wx[s], 3 * (n + 1) + 1)
                        for h in range(2):
                            if s:
                                pe.wait_ge(s_vac[0], 2 * n + h + 2)
                            else:
                                pe.wait_ge(s_vac[1], 2 * n + 1)
                                pe.wait_ge(s_lr[1], 2 * (p + 1))
                            for g in range(2):
                                b = 2 * h + g
                                o = ps_v[h][:, g * VW:(g + 1) * VW]
                                mm(o, xc[s][:, b * N:(b + 1) * N], wx[s][:, b, 0, :], stop=False, skip_group_check=True)
                                last = mm(o, prod[s][:, b * N:(b + 1) * N], wx[s][:, b, 1, :], start=False, skip_group_check=True)
                            last.then_inc(s_vp[s], 1)
                    for s in range(SETS):
                        pe.wait_ge(s_spl[s], n + 1)
                        if s:
                            pe.wait_ge(s_at[0], n + 1)
                        else:
                            pe.wait_ge(s_xx[1], n + 1)
                        nc.tensor.transpose(ps_act, parts[s][:, :, :].rearrange("p b c -> p (b c)"), identb).then_inc(s_ap[s], 1)
                        pe.wait_ge(s_at[s], n + 1)
                        pe.wait_ge(s_eq[s], TYPES * (p + 1) + 1)
                        for b in range(SG):
                            if b >= 2:
                                pe.wait_ge(s_sm[s], SG * n + b)
                            elif s:
                                pe.wait_ge(s_sm[0], SG * n + b + 4)
                            else:
                                pe.wait_ge(s_sm[1], SG * n + 1)
                            o = ps_s[b % 2]
                            mm(o[:, :], acT[s][:, :], selA[:, b, :], stop=False)
                            for r in range(TYPES):
                                mm(o[:, r * N:(r + 1) * N], selC[:, b, r, :], acT[s][:, :], start=False, stop=False)
                            mm(o[:, :], negid, eqn[s][:, b, :, :].rearrange("p r j -> p (r j)"), start=False).then_inc(s_s[s], 1)

                    def transposes(s):
                        if s:
                            pe.wait_ge(s_pt[0], n + 2)
                        else:
                            pe.wait_ge(s_pt[1], n + 1)
                        for b in range(SG):
                            pe.wait_ge(s_pn[s], SG * n + b + 1)
                            last = nc.tensor.transpose(ps_pt[:, b * N:(b + 1) * N], pn[s][:, b, :], ident[:, :])
                        last.then_inc(s_ptp[s], 1)

                    def mu_first(s):
                        if s:
                            pe.wait_ge(s_xx[0], n + 2)
                        mm(ps_mu[:, :], w("mu0T"), xc[s][:, :], stop=False)

                    def message(s):
                        pe.wait_ge(s_pt[s], n + 2)
                        if s:
                            pe.wait_ge(s_mg[0], n + 2)
                        else:
                            pe.wait_ge(s_mg[1], n + 1)
                        for b in range(SG):
                            last = mm(ps_msg[:, b * N:(b + 1) * N], vac[s][:, b, 0:D], pT[s][:, b, :])
                        last.then_inc(s_mp[s], 1)

                    def mu_second(s):
                        pe.wait_ge(s_mg[s], n + 2)
                        mm(ps_mu[:, :], w("mu1T"), msg[s][:, :, :].rearrange("p b i -> p (b i)"), start=False).then_inc(s_mu[s], 1)

                    transposes(0)
                    pe.wait_ge(s_at[1], n + 1)
                    mu_first(0)
                    message(0)
                    transposes(1)
                    mu_second(0)
                    message(1)
                    mu_first(1)
                    mu_second(1)
                for s in range(SETS):
                    if s:
                        pe.wait_ge(s_xm[0], p + 2)
                    else:
                        pe.wait_ge(s_prod[1], T * (p + 1) + 1)
                    pe.wait_ge(s_xx[s], T * (p + 1) + 1)
                    mm(ps_pc[:, :], w("cb0T"), xs[s][:, :], stop=False)
                    mm(ps_pc[:, :], w("cb1T"), xctx[s][:, :], start=False).then_inc(s_cb[s], 1)
                for s in range(SETS):
                    pe.wait_ge(s_xm[s], p + 2)
                    pe.wait_ge(s_vac[1], 2 * T * (p + 1) + 1)
                    for b in range(SG):
                        last = mm(ps_v[s][:, b * E:(b + 1) * E], xm[s][:, b * N:(b + 1) * N], w("gateT", E))
                    last.then_inc(s_gp[s], 1)

            pe.wait_ge(s_fw, 64)
            pe.wait_ge(s_xa, 2 * PAIRS + 1)
            pe.wait_ge(s_gwork, GATE_OPS)
            with pe.Fori(0, TT) as q:
                pe.wait_ge(s_gc, q + 1)
                for b in range(SG):
                    last = nc.tensor.transpose(PS[6][0:E, b * 128:(b + 1) * 128], gcur[:, b, :], ident[:, :])
                last.then_inc(s_gtp, 1)
                pe.wait_ge(s_gt, q + 1)
                for b in range(SG):
                    last = mm(PS[7][:, b * D:(b + 1) * D], gT[:, b * 128:(b + 1) * 128], b2s[:, :])
                last.then_inc(s_b2, 1)

                def hidden(e):
                    for c in range(FC):
                        if e:
                            pe.wait_ge(s_h[c], q * E + e + 1)
                        else:
                            pe.wait_ge(s_h[c], q * E + 1)
                        mm(PS[c][:, :], w1s[:, e, c * 128:(c + 1) * 128], xmall[:, bass.ds(q * ST, ST)]).then_inc(s_hp[c], 1)

                def output(e):
                    if e >= 2:
                        pe.wait_ge(s_acc, (q * E + e - 1) * SG + 1)
                    else:
                        pe.wait_ge(s_acc, q * E * SG + 1)
                    for c in range(FC):
                        pe.wait_ge(s_h[c], q * E + e + 2)
                    for b in range(SG):
                        for c in range(FC):
                            last = mm(PS[4 + e % 2][:, b * D:(b + 1) * D], hT[e % 2][:, c, b * 128:(b + 1) * 128],
                                      w2s[:, e, c, :], start=c == 0, stop=c == FC - 1)
                    last.then_inc(s_yp, 1)

                hidden(0)
                for e in range(E):
                    if e + 1 < E:
                        hidden(e + 1)
                    output(e)

        @block.scalar
        def _(act):
            def actv(o, i, f, **k):
                return nc.scalar.activation(o, i, f, **k)

            act.wait_ge(s_w, 80)
            act.wait_ge(s_q, 2)
            actv(qb_e[:, :], qb_e[:, :], ACT.Exp).then_inc(s_pe_, 1)
            act.wait_ge(s_pp, 2)
            for t in range(T):
                last = actv(cmd[:, t * B:(t + 1) * B], PS[1][:, t * B:(t + 1) * B], ACT.Identity, bias=W[:, WOFF["b_qt"] + t:WOFF["b_qt"] + t + 1])
            last.then_inc(s_pe_, 1)
            with act.Fori(0, PAIRS) as p:
                for s in range(SETS):
                    act.wait_ge(s_pl[s], p + 1)
                    actv(pl[s][:, :], ps_pc[:, :], ACT.Identity, bias=w("b_pl", 1)).then_inc(s_plr[s], 1)
                with act.Fori(0, T) as t:
                    n = p * T + t
                    for s in range(SETS):
                        act.wait_ge(s_ap[s], n + 1)
                        actv(acT[s][:, :], ps_act, ACT.Copy).then_inc(s_at[s], 1)
                    for s in range(SETS):
                        act.wait_ge(s_lk[s], n + 1)
                        for b in range(SG):
                            actv(pr[s][:, b, :], lk[s][:, b, :], ACT.Exp, bias=nm[s][:, b:b + 1],
                                 accum_out=rs[s][:, b:b + 1]).then_inc(s_ex[s], 1)
                        act.wait_ge(s_ptp[s], n + 1)
                        actv(pT[s][:, :, :], ps_pt[:, :].rearrange("p (b i) -> p b i", b=SG), ACT.Copy).then_inc(s_pt[s], 1)
                    for s in range(SETS):
                        act.wait_ge(s_mu[s], n + 1)
                        act.wait_ge(s_xc[s], p * (T + 1) + t + 2)
                        actv(xctx[s][:, :], ps_mu[:, :], ACT.Identity, bias=w("b_mu", 1)).then_inc(s_xx[s], 1)
                for s in range(SETS):
                    act.wait_ge(s_cb[s], p + 2)
                    act.wait_ge(s_xa, 2 * p + 1)
                    actv(xm[s][:, :], ps_pc[:, :], ACT.Identity, bias=w("b_cb", 1)).then_inc(s_xm[s], 1)
                for s in range(SETS):
                    act.wait_ge(s_gp[s], p + 1)
                    actv(lg[:, bass.ds((p * SETS + s) * SG, SG), :], ps_v[s][:, 0:SG * E].rearrange("p (b e) -> p b e", b=SG), ACT.Copy).then_inc(s_lg[s], 1)
            act.wait_ge(s_gx, 1)
            actv(g1[:, :, :], g1[:, :, :], ACT.Exp).then_inc(s_exg, 1)
            with act.Fori(0, TT) as q:
                act.wait_ge(s_gtp, q + 2)
                actv(gT[:, :], PS[6][0:E, :], ACT.Copy).then_inc(s_gt, 1)
                for e in range(E):
                    for c in (0, 2):
                        act.wait_ge(s_hp[c], q * E + e + 1)
                        if e >= 2:
                            act.wait_ge(s_yp, q * E + e)
                        else:
                            act.wait_ge(s_yp, q * E + 1)
                        actv(hT[e % 2][:, c, :], PS[c][:, :], ACT.Relu, bias=b1s[:, e * FC + c:e * FC + c + 1]).then_inc(s_h[c], 1)

        @block.gpsimd
        def _(pool):
            g = nc.gpsimd
            pool.wait_ge(s_pv_, 3)
            with pool.Fori(0, PAIRS) as p:
                with pool.Fori(0, T) as t:
                    n = p * T + t
                    for s in range(SETS):
                        pool.wait_ge(s_vp[s], 2 * n + 1)
                        pool.wait_ge(s_vac[s], 2 * n + 1)
                        pool.wait_ge(s_lr[s], 2 * (p + 1))
                        g.tensor_copy(loc[s][:, :, D + TYPES:].unsqueeze(2), locC[s][:, :, bass.ds(t, 1), :]).then_inc(s_wx[s], 1)
                        for c in range(2):
                            g.tensor_copy(wx[s][:, :, c, D + TYPES:],
                                          Kef[:, c + 1, bass.ds((p * SETS + s) * SG, SG), bass.ds(t * TYPES, TYPES)]).then_inc(s_wx[s], 1)
                    for s in range(SETS):
                        pool.wait_ge(s_xx[s], n + 2)
                        pool.wait_ge(s_mu[s], n + 1)
                        g.tensor_tensor(xc[s][:, :], xctx[s][:, :], mk[s][:, :], ALU.mult).then_inc(s_xc[s], 1)

        @block.vector
        def _(dve):
            v = nc.vector

            dve.wait_ge(s_w, 80)
            dve.wait_ge(s_pp, 1)
            v.tensor_scalar(qb_r[:, :], PS[0][:, 0:B], w("b_qin", 1), 0.0, ALU.add, ALU.max).then_inc(s_q, 1)
            v.tensor_scalar(qb_e[:, :], PS[0][:, 0:B], w("b_qin", 1), 0.0, ALU.add, ALU.min).then_inc(s_q, 1)
            for s in range(SETS):
                for b in range(SG):
                    for c in range(2):
                        v.tensor_copy(wx[s][:, b, c, 0:D], w(f"v{c + 1}T"))
                v.memset(parts[s][:, :, :], 0.0)
            dve.wait_ge(s_pe_, 1)
            dve.wait_ge(s_q, 2)
            v.scalar_tensor_tensor(qbase[:, :], qb_e[:, :], -1.0, qb_r[:, :], ALU.add, ALU.add).then_inc(s_pv_, 1)
            dve.wait_ge(s_pp, 3)
            v.tensor_scalar(ck[:, :], PS[2][:, 0:TB], w("b_pk", 1), None, ALU.add).then_inc(s_cvr, 1)
            v.tensor_scalar(cv[:, :], PS[2][:, TB:2 * TB], w("b_pv", 1), None, ALU.add).then_inc(s_cvr, 1)
            dve.wait_ge(s_cvr, 2)
            for i in range(TYPES):
                last = v.tensor_scalar(KW[:, :, i], ck[:, :], W[:, WOFF["w2T"] + i:WOFF["w2T"] + i + 1], None, ALU.mult)
            last.then_inc(s_pv_, 1)
            dve.wait_ge(s_pp, 4)
            for c in range(3):
                v.tensor_copy(Kef[:, c, :, :].rearrange("p b (t i) -> p b t i", t=T),
                              PS[3 + c][:, :].rearrange("p (t b i) -> p b t i", t=T, b=B))
            v.tensor_copy(Q[:, :, :], PS[6][:, 0:3 * TYPES].rearrange("p (c i) -> p c i", c=3))
            v.tensor_copy(bcst[:, 0:TYPES], PS[6][:, 16:16 + TYPES])
            v.tensor_copy(bcst[:, TYPES:].rearrange("p (b t i) -> p b t i", b=B, t=T),
                          PS[7][:, :].rearrange("p (t b i) -> p b t i", t=T, b=B)).then_inc(s_cvr, 1)
            dve.wait_ge(s_cvr, 3)
            for s in range(SETS):
                for b in range(SG):
                    last = v.tensor_copy(wx[s][:, b, :, D:D + TYPES], Q[:, 1:3, :])
            last.then_inc(s_pv_, 1)

            with dve.Fori(0, PAIRS) as p:
                for s in range(SETS):
                    first = (p * SETS + s) * SG
                    dve.wait_ge(s_x[s], 48 * (p + 1))
                    dve.wait_ge(s_cb[s], p + 1)
                    dve.wait_ge(s_xc[s], p * (T + 1) + 1)
                    v.tensor_scalar(xc[s][:, :], mk[s][:, :], w("init", 1), None, ALU.mult).then_inc(s_xc[s], 1)
                for s in range(SETS):
                    first = (p * SETS + s) * SG
                    for h in range(2):
                        dve.wait_ge(s_lp[s], 2 * p + h + 1)
                        dve.wait_ge(s_wx[s], 3 * T * p + 1)
                        o = ps_v[h][:, :].rearrange("p (g c) -> p g c", g=2)
                        bs = slice(2 * h, 2 * h + 2)
                        v.tensor_tensor(loc[s][:, bs, 0:D], o[:, :, 0:D], bv[:, :].unsqueeze(1).to_broadcast([128, 2, D]), ALU.add)
                        v.tensor_tensor(loc[s][:, bs, D:D + TYPES], o[:, :, D:D + TYPES],
                                        bcst[:, 0:TYPES].unsqueeze(1).to_broadcast([128, 2, TYPES]), ALU.add)
                        v.tensor_tensor(locC[s][:, bs, :, :].rearrange("p b t i -> p b (t i)"), o[:, :, D + TYPES:D + TYPES * (1 + T)],
                                        bcst[:, TYPES:].rearrange("p (b c) -> p b c", b=B)[:, bass.ds(first + 2 * h, 2), :], ALU.add).then_inc(s_lr[s], 1)
                for s in range(SETS):
                    for r in range(TYPES):
                        v.tensor_scalar(eqn[s][:, :, r, :], ad[s][:, :, :], r + 1, None, ALU.not_equal).then_inc(s_eq[s], 1)

                with dve.Fori(0, T) as t:
                    n = p * T + t
                    for s in range(SETS):
                        dve.wait_ge(s_pc[s], n + 1)
                        dve.wait_ge(s_plr[s], p + 1)
                        v.scalar_tensor_tensor(prod[s][:, :], ps_pc[:, :], w("b_pc", 1), pl[s][:, :], ALU.add, ALU.mult).then_inc(s_prod[s], 1)
                    for s in range(SETS):
                        for h in range(2):
                            dve.wait_ge(s_vp[s], 2 * n + h + 2)
                            bs = slice(2 * h, 2 * h + 2)
                            v.tensor_tensor(vac[s][:, bs, :], ps_v[h][:, 0:2 * VW].rearrange("p (g c) -> p g c", g=2),
                                            loc[s][:, bs, :], ALU.add).then_inc(s_vac[s], 1)
                        score = vac[s][:, :, D:]
                        dve.wait_ge(s_vac[s], 2 * (n + 1) + 1)
                        v.tensor_copy(parts[s][:, :, 0:AC], score).then_inc(s_st[s], 1)
                        dve.wait_ge(s_st[s], 3 * n + 1)
                        v.tensor_tensor(rest[s][:, :, :], score, parts[s][:, :, 0:AC], ALU.subtract).then_inc(s_st[s], 1)
                        dve.wait_ge(s_st[s], 3 * n + 2)
                        v.tensor_copy(parts[s][:, :, AC:2 * AC], rest[s][:, :, :]).then_inc(s_st[s], 1)
                        dve.wait_ge(s_st[s], 3 * n + 3)
                        v.tensor_tensor(parts[s][:, :, 2 * AC:3 * AC], rest[s][:, :, :], parts[s][:, :, AC:2 * AC], ALU.subtract).then_inc(s_spl[s], 1)

                    def edge(s, b):
                        dve.wait_ge(s_s[s], SG * n + b + 1)
                        v.tensor_reduce(sc[s][:, b, :], ps_s[b % 2][:, :].rearrange("p (r j) -> p j r", r=TYPES),
                                        AX.X, ALU.max).then_inc(s_sm[s], 1)

                    def logits(s):
                        dve.wait_ge(s_sm[s], SG * (n + 1) + 1)
                        v.scalar_tensor_tensor(lk[s][:, :, :], sc[s][:, :, :], ALPHA, sc[s][:, :, :], ALU.mult, ALU.max).then_inc(s_le[s], 1)
                        dve.wait_ge(s_le[s], n + 1)
                        v.tensor_reduce(nm[s][:, :], lk[s][:, :, :], AX.X, ALU.max, negate=True).then_inc(s_lk[s], 1)

                    def probs(s, h):
                        dve.wait_ge(s_ex[s], SG * n + 2 * h + 2)
                        v.reciprocal(ri[s][:, 2 * h:2 * h + 2], rs[s][:, 2 * h:2 * h + 2]).then_inc(s_ri[s], 1)
                        dve.wait_ge(s_ri[s], 2 * n + h + 1)
                        for b in (2 * h, 2 * h + 1):
                            v.tensor_scalar(pn[s][:, b, :], pr[s][:, b, :], ri[s][:, b:b + 1], None, ALU.mult).then_inc(s_pn[s], 1)

                    def message(s):
                        dve.wait_ge(s_mp[s], n + 1)
                        c = cv[:, bass.ds(t * B + (p * SETS + s) * SG, SG)].unsqueeze(2).to_broadcast([128, SG, N])
                        v.tensor_tensor(msg[s][:, :, :], ps_msg[:, :].rearrange("p (b i) -> p b i", b=SG), c, ALU.mult).then_inc(s_mg[s], 1)

                    for b in range(SG):
                        edge(0, b)
                    logits(0)
                    edge(1, 0)
                    edge(1, 1)
                    probs(0, 0)
                    edge(1, 2)
                    probs(0, 1)
                    edge(1, 3)
                    logits(1)
                    message(0)
                    probs(1, 0)
                    probs(1, 1)
                    message(1)
                for s in range(SETS):
                    dve.wait_ge(s_xm[s], p + 2)
                    v.tensor_copy(xmall[:, bass.ds((p * SETS + s) * ST, ST)], xm[s][:, :]).then_inc(s_xa, 1)

            def bc(a):
                return a[:, :].unsqueeze(2).to_broadcast([128, NT, E])
            rk = rank[:, :].unsqueeze(1).to_broadcast([128, NT, E])
            steps = [0]

            def link(ins):
                ins.then_inc(s_gwork, 1)
                steps[0] += 1
                dve.wait_ge(s_gwork, steps[0])

            dve.wait_ge(s_lg[1], PAIRS + 1)
            link(v.tensor_reduce(gm[:, :], lg[:, :, :], AX.X, ALU.max))
            v.tensor_tensor(g1[:, :, :], lg[:, :, :], bc(gm), ALU.subtract).then_inc(s_gx, 1)
            dve.wait_ge(s_exg, 1)
            link(v.tensor_reduce(gm[:, :], g1[:, :, :], AX.X, ALU.add))
            link(v.reciprocal(gm[:, :], gm[:, :]))
            link(v.tensor_tensor(g1[:, :, :], g1[:, :, :], bc(gm), ALU.mult))

            def pick(prob, sel):
                link(v.tensor_reduce(gm[:, :], prob[:, :, :], AX.X, ALU.max))
                link(v.tensor_tensor(g3[:, :, :], prob[:, :, :], bc(gm), ALU.is_equal))
                link(v.tensor_tensor(g3[:, :, :], g3[:, :, :], rk, ALU.mult))
                link(v.tensor_reduce(gm[:, :], g3[:, :, :], AX.X, ALU.max))
                link(v.tensor_tensor(sel[:, :, :], g3[:, :, :], bc(gm), ALU.is_equal))

            pick(g1, gsel)
            link(v.scalar_tensor_tensor(g2[:, :, :], gsel[:, :, :], -2.0, g1[:, :, :], ALU.mult, ALU.add))
            pick(g2, gates)
            link(v.tensor_tensor(gsel[:, :, :], gsel[:, :, :], gates[:, :, :], ALU.add))
            link(v.tensor_tensor(gates[:, :, :], gsel[:, :, :], g1[:, :, :], ALU.mult))
            assert steps[0] == GATE_OPS, steps[0]

            with dve.Fori(0, TT) as q:
                dve.wait_ge(s_gtp, q + 1)
                v.tensor_copy(gcur[:, :, :], gates[:, bass.ds(q * SG, SG), :]).then_inc(s_gc, 1)
                dve.wait_ge(s_b2, q + 1)
                dve.wait_ge(s_xr, 16 * (q + 1))
                dve.wait_ge(s_out, 16 * q + 1)
                v.tensor_tensor(acc[0][:, :, :], PS[7][:, :].rearrange("p (b d) -> p b d", b=SG), xres[:, :, :], ALU.add).then_inc(s_acc0, 1)

                def hidden(e):
                    for c in (1, 3):
                        dve.wait_ge(s_hp[c], q * E + e + 1)
                        if e >= 2:
                            dve.wait_ge(s_yp, q * E + e)
                        else:
                            dve.wait_ge(s_yp, q * E + 1)
                        v.tensor_scalar(hT[e % 2][:, c, :], PS[c][:, :], b1s[:, e * FC + c:e * FC + c + 1], 0.0, ALU.add, ALU.max).then_inc(s_h[c], 1)

                hidden(0)
                for e in range(E):
                    if e + 1 < E:
                        hidden(e + 1)
                    dve.wait_ge(s_yp, q * E + e + 2)
                    if e:
                        dve.wait_ge(s_acc, (q * E + e) * SG + 1)
                    else:
                        dve.wait_ge(s_acc0, q + 2)
                    for b in range(SG):
                        a = acc[0][:, b, :]
                        v.scalar_tensor_tensor(a, PS[4 + e % 2][:, b * D:(b + 1) * D], gates[:, bass.ds(q * SG + b, 1), e], a,
                                               ALU.mult, ALU.add).then_inc(s_acc, 1)


def kernel(**inputs):
    import numpy as np
    import ml_dtypes
    import concourse.bacc as bacc
    from concourse.bass_utils import run_bass_kernel_spmd

    a = {k: np.asarray(v) for k, v in inputs.items()}
    c = {k[8:]: v for k, v in a.items() if k.startswith("L0_cond_")}
    f = {k[7:]: v for k, v in a.items() if k.startswith("L0_ffn_")}
    steps = a["fside_BxSxS_0"][:STEPS]
    wes = a["cond_2048"]
    cols = ([c["w_qin"].T] + [steps[t].T for t in range(STEPS)] + [c["w_pk"].T, c["w_pv"].T]
            + [c["w_k"], c["w_q"], c["w_pl"].T, c["w_pc"].T]
            + [c["w_v"][:, i * D:(i + 1) * D].T for i in range(3)]
            + [c["w_mu"][:, i * D:(i + 1) * D].T for i in range(2)]
            + [c["w_cb"][:, i * D:(i + 1) * D].T for i in range(2)]
            + [f["gate_w"].T, wes[:TYPES, :D].T, wes[:TYPES, D:].T, a["mask_BxS_ff0"][:STEPS].T]
            + [c[k].reshape(D, 1) for k in ("b_qin", "b_pl", "b_pc", "b_q", "b_k", "b_pk", "b_pv", "b_mu", "b_cb")]
            + [c["init_mem"].reshape(D, 1)])
    sel_a = np.zeros((SG, 32, SG, TYPES, N), np.float32)
    sel_c = np.zeros((SG, 32, SG, TYPES, N), np.float32)
    for b in range(SG):
        for part in range(3):
            for r in range(TYPES):
                sel_a[b, part * AC + r, b, r, :] = 1
                sel_c[b, part * AC + TYPES + r, b, r, :] = 1
    eye = np.eye(128, dtype=np.float32)
    consts = np.concatenate([eye, -BIG * eye, sel_a.reshape(128, -1), sel_c.reshape(128, -1)], 1).astype(ml_dtypes.bfloat16)
    arrays = {
        "xT": a["x"].reshape(TOK, D).T, "x": a["x"], "mask": a["mask_BxS_ff1"].reshape(TOK), "adj": a["itok_BxSxS_0_4"],
        "fsT": a["fside_BxS_0"].T, "wpack": np.concatenate(cols, 1), "bvrow": c["b_v"],
        "w1": f["w1"].transpose(1, 0, 2), "b1T": f["b1"].reshape(E * FC, 128).T,
        "w2": f["w2"].reshape(E, FC, 128, D).transpose(2, 0, 1, 3), "b2": f["b2"],
        "ident_d": np.concatenate([eye, np.tile(np.arange(E, 0, -1, dtype=np.float32), (128, 1))], 1), "bf_d": consts,
    }
    nc = bacc.Bacc("TRN2", target_bir_lowering=False, num_devices=1)
    args = {}
    for name, arr in list(arrays.items()):
        arrays[name] = arr = np.ascontiguousarray(arr)
        args[name] = nc.dram_tensor(name, arr.shape, mybir.dt.from_np(arr.dtype), kind="ExternalInput").ap()
    args["out"] = nc.dram_tensor("out", (B, N, D), mybir.dt.float32, kind="ExternalOutput").ap()
    build(nc, **args)
    return run_bass_kernel_spmd(nc, [arrays], core_ids=[0]).results[0]["out"]
```

```python
import concourse.bass as bass
from concourse import mybir
from contextlib import ExitStack

B, N, D = 32, 128, 128
TOK = B * N
STEPS = 4
TYPES = 4
E, F = 8, 512
FC = F // 128
UG = 2
UNITS = 4
GROUPS = B // (UG * UNITS)
UT = UG * N
SG = 4
NT = TOK // 128
KTOP = 2
MT = -(-(KTOP * TOK // 128 + E - 1) // 8) * 8
ALPHA = 0.2
BIG = 9000000000000000.0
AC = 2 * TYPES
VW = D + AC

WNAMES = (["qinT"] + [f"qtT{t}" for t in range(STEPS)] + ["pkT", "pvT"] + ["k0", "k1", "k2", "q0", "q1", "q2"]
          + ["plT", "pcT", "v0T", "v1T", "v2T", "mu0T", "mu1T", "cb0T", "cb1T"])
SMALL = [("gateT", E), ("w1T", TYPES), ("w2T", TYPES), ("b_qt", STEPS)] + [
    (b, 1) for b in ("b_qin", "b_pl", "b_pc", "b_q", "b_k", "b_pk", "b_pv", "b_mu", "b_cb", "init")]
WOFF = {}
WCOLS = 0
for _n, _w in SMALL + [(w, D) for w in WNAMES]:
    WOFF[_n] = WCOLS
    WCOLS += _w
COMMAND_COLS = WOFF["k0"]


def build(nc, xT, x, mask, adj, fsT, wpack, bvrow, w1, b1, w2, b2, ident_d, bf_d, rcf_d, rcb_d, out):
    fp32, bf16, i32 = mybir.dt.float32, mybir.dt.bfloat16, mybir.dt.int32
    ALU = mybir.AluOpType
    ACT = mybir.ActivationFunctionType
    AX = mybir.AxisListType
    TB = STEPS * B

    ctx = ExitStack()
    with ctx:
        def sb(name, shape, dt=fp32):
            return ctx.enter_context(nc.sbuf_tensor(name, shape, dt))

        def sem(name):
            return ctx.enter_context(nc.semaphore(name))

        W = sb("W", [128, WCOLS])

        def w(name, width=D):
            return W[:, WOFF[name]:WOFF[name] + width]

        bv = sb("bv", [128, D])
        idr = sb("idr", [128, 128 + E])
        ident = idr[:, 0:128]
        rank = idr[:, 128:]
        BFC = 256 + UG * TYPES * 128 * 2
        bfc = sb("bfc", [128, BFC], bf16)
        identb = bfc[:, 0:128]
        negid = bfc[:, 128:256]
        selA = bfc[:, 256:256 + UG * TYPES * 128].rearrange("p (b c) -> p b c", b=UG)
        selC = bfc[:, 256 + UG * TYPES * 128:].rearrange("p (b r i) -> p b r i", b=UG, r=TYPES)
        Q = sb("Q", [128, 3, TYPES])
        v0q = sb("v0q", [128, D + TYPES])
        fs = sb("fs", [128, B])
        warm = sb("warm", [128, 1])
        qb_e = sb("qb_e", [128, B])
        qb_r = sb("qb_r", [128, B])
        qbase = sb("qbase", [128, B])
        cmd = sb("cmd", [128, TB])
        ck = sb("ck", [128, TB])
        cv = sb("cv", [128, TB])
        KW = sb("KW", [128, TB, TYPES])
        Kef = sb("Kef", [128, 3, B, STEPS * TYPES])
        bcst = sb("bcst", [128, TYPES + B * STEPS * TYPES])
        units = range(UNITS)
        xs = [sb(f"xs{u}", [128, UT]) for u in units]
        mk = [sb(f"mk{u}", [128, UT]) for u in units]
        ad = [sb(f"ad{u}", [128, UG, N], i32) for u in units]
        eqn = [sb(f"eqn{u}", [128, UG, TYPES, N], bf16) for u in units]
        pl = [sb(f"pl{u}", [128, UT]) for u in units]
        cbx = [sb(f"cbx{u}", [128, UT]) for u in units]
        xc = [sb(f"xc{u}", [128, UT]) for u in units]
        xctx = [sb(f"xctx{u}", [128, UT]) for u in units]
        prod = [sb(f"prod{u}", [128, UT]) for u in units]
        wx = [sb(f"wx{u}", [128, UG, 2, VW]) for u in units]
        loc = [sb(f"loc{u}", [128, UG, VW]) for u in units]
        locC = [sb(f"locC{u}", [128, UG, STEPS, TYPES]) for u in units]
        vac = [sb(f"vac{u}", [128, UG, VW]) for u in units]
        rest = [sb(f"rest{u}", [128, UG, AC]) for u in units]
        parts = [sb(f"parts{u}", [128, 4, 32], bf16) for u in units]
        acT = [sb(f"acT{u}", [128, 128], bf16) for u in units]
        sc = [sb(f"sc{u}", [128, UG, N]) for u in units]
        nm = [sb(f"nm{u}", [128, UG]) for u in units]
        rs = [sb(f"rs{u}", [128, UG]) for u in units]
        ri = [sb(f"ri{u}", [128, UG]) for u in units]
        pr = [sb(f"pr{u}", [128, UG, N]) for u in units]
        pn = [sb(f"pn{u}", [128, UG, N]) for u in units]
        pT = [sb(f"pT{u}", [128, UG, N]) for u in units]
        msg = [sb(f"msg{u}", [128, UG, N]) for u in units]
        xm = [sb(f"xm{u}", [128, UT]) for u in units]
        lg = sb("lg", [128, NT, E])
        g1 = sb("g1", [128, NT, E])
        g2 = sb("g2", [128, NT, E])
        g3 = sb("g3", [128, NT, E])
        sel1 = sb("sel1", [128, NT, E])
        sel2 = sb("sel2", [128, NT, E])
        selb = sb("selb", [128, NT, E], bf16)
        gm = sb("gm", [128, NT])
        gp = sb("gp", [128, NT])
        gk = sb("gk", [128, NT, KTOP])
        cntb = sb("cntb", [128, 2], bf16)
        ti = sb("ti", [128, E], i32)
        tf = sb("tf", [128, E])
        t88 = sb("t88", [128, E, E])
        tb = sb("tb", [128, E])
        tge = sb("tge", [1, MT, E - 1])
        tef = sb("tef", [1, MT])
        tep = sb("tep", [1, MT // 8])
        te = sb("te", [1, MT // 8], i32)
        pos = sb("pos", [128, NT, KTOP])
        posi = sb("posi", [128, NT, KTOP], i32)
        hii = sb("hii", [128, NT, KTOP], i32)
        loi = sb("loi", [128, NT, KTOP], i32)
        OC = 8
        lob = sb("lob", [128, NT * KTOP], bf16)
        hib = sb("hib", [128, NT * KTOP], bf16)
        ohl = [sb(f"ohl{j}", [128, OC, 128], bf16) for j in range(2)]
        ohh = [sb(f"ohh{j}", [128, OC, MT], bf16) for j in range(2)]
        ohr = [sb(f"ohr{j}", [128, OC, 2, MT], bf16) for j in range(2)]
        zero = sb("zero", [128, 2 * MT], bf16)
        slot = sb("slot", [128, MT])
        none = sb("none", [128, MT])
        rows = sb("rows", [128, MT // 4 + 2, 2, 4], i32)
        rows_c = [sb(f"rows_c{h}", [128, 2, 4], i32) for h in range(2)]
        rcf = sb("rcf", [128, 128 + 1 + E * E])
        rf_iota = rcf[:, 0:128]
        rf_place = rcf[:, 128:129]
        rf_tri = rcf[:, 129:].rearrange("p (a b) -> p a b", a=E)
        RB = 128 + 2 * NT * E + 2 * E + 1
        rcb = sb("rcb", [128, RB + 128 + NT * KTOP], bf16)
        rb_iota = rcb[:, RB:RB + 128]
        rb_num = rcb[:, RB + 128:]
        rc_tri = rcb[:, 0:128]
        rc_m = rcb[:, 128:128 + 2 * NT * E].rearrange("p (h c) -> p h c", h=2)
        rc_t = rcb[:, 128 + 2 * NT * E:128 + 2 * NT * E + 2 * E].rearrange("p (h c) -> p h c", h=2)
        rc_one = rcb[:, RB - 1:RB]
        xrow = [sb(f"xrow{i}", [128, UG, D]) for i in range(2)]
        w1s = sb("w1s", [128, E, F])
        w2s = sb("w2s", [128, E, FC, D])
        b1s = sb("b1s", [128, E, F])
        b2s = sb("b2s", [128, E, D])
        xg = [sb(f"xg{j}", [128, D]) for j in range(4)]
        xt = [sb(f"xt{j}", [128, 128]) for j in range(2)]
        hb = [sb(f"hb{j}", [128, F]) for j in range(2)]
        hT = [sb(f"hT{j}", [128, F]) for j in range(2)]
        yb = [sb(f"yb{j}", [128, D]) for j in range(4)]
        KF = Kef[:, :, :, :].rearrange("p c b i -> p (c b i)")
        XW = SG * D
        xres = [(W[:, q * XW:(q + 1) * XW] if q < 5 else KF[:, (q - 5) * XW:(q - 4) * XW]).rearrange("p (b d) -> p b d", b=SG)
                for q in range(NT // SG)]
        YW = SG * KTOP * D
        w1f = w1s[:, :, :].rearrange("p e f -> p (e f)")
        w2f = w2s[:, :, :, :].rearrange("p e c d -> p (e c d)")
        yin = [(w1f[:, q * YW:(q + 1) * YW] if q < 4 else w2f[:, (q - 4) * YW:(q - 3) * YW]).rearrange(
            "p (b k d) -> p b k d", b=SG, k=KTOP) for q in range(NT // SG)]
        xm_s = nc.dram_tensor("xm_rows", [128, NT, D], fp32, kind="Internal").ap()
        xm_d = xm_s.rearrange("p t d -> (p t) d")
        y_s = nc.dram_tensor("expert_rows", [128, NT, KTOP, D], fp32, kind="Internal").ap()
        y_d = y_s.rearrange("p t k d -> (p t k) d")

        PS = [ctx.enter_context(nc.psum_tensor(f"ps{i}", [128, 512], fp32)) for i in range(8)]
        ps_pc, ps_v, ps_s, ps_pt, ps_msg, ps_mu, ps_x = PS[0], PS[1], PS[2:4], PS[4], PS[5], PS[6], PS[7]
        ps_act = ps_msg[:, :].bitcast(bf16)[:, 0:128]
        CC = TYPES * (1 + STEPS)

        s_w = sem("command_weights_loaded")
        s_w2 = sem("weights_and_constants_loaded")
        s_fw = sem("expert_weights_loaded")
        s_pp = sem("setup_product")
        s_pe_ = sem("setup_scalar_done")
        s_pv_ = sem("setup_vector_done")
        s_kc = sem("last_key_vectors_ready")
        s_warm = sem("exp_argument_ready")
        s_x = [sem(f"unit_loaded_{u}") for u in units]
        s_lp = sem("local_product")
        s_lr = sem("local_ready")
        s_plp = sem("gate_projection")
        s_pl = sem("gate_projection_ready")
        s_cxp = sem("local_combined_product")
        s_cx = sem("local_combined_ready")
        s_eq = sem("edge_masks_ready")
        s_xc0 = sem("first_context_ready")
        s_pc = sem("context_product")
        s_prod = sem("gated_product_ready")
        s_wx = sem("value_weights_ready")
        s_vp = sem("value_product")
        s_vac = sem("value_ready")
        s_st = sem("score_split_steps")
        s_spl = sem("score_parts_ready")
        s_ap = sem("score_transposed")
        s_at = sem("score_rows_ready")
        s_s = sem("edge_scores")
        s_sm = sem("edge_scores_read")
        s_le = sem("leaky_done")
        s_lk = sem("logits_ready")
        s_ex = sem("exp_done")
        s_ri = sem("row_sum_inverse")
        s_pn = sem("probs_ready")
        s_ptp = sem("probs_transposed")
        s_pt = sem("probs_T_ready")
        s_mp = sem("message_product")
        s_mg = sem("message_ready")
        s_mu = sem("update_product")
        s_mur = sem("context_updated")
        s_cb = sem("combined_product")
        s_xm = sem("combined_ready")
        s_gr = sem("gate_and_row_product")
        s_grr = sem("gate_and_row_read")
        s_q = sem("query_base_steps")
        s_cvr = sem("value_command_ready")
        s_exg = sem("gate_exp_done")
        s_gx = sem("gate_max_subtracted")
        s_ga = sem("gates_ready")

        T = STEPS

        s_xs = [sem(f"rows_stored_{j}") for j in range(2)]
        s_gwork = sem("gate_steps")
        s_sel = sem("choices_ready")
        s_rp = sem("routing_product")
        s_cnt = sem("tile_counts_ready")
        s_te = sem("tile_experts_ready")
        s_oh = sem("one_hots_ready")
        s_ohp = sem("one_hots_read")
        s_ohh = sem("tile_one_hots_ready")
        s_ohg = sem("tile_one_hots_by_column_ready")
        s_oha = sem("tile_one_hots_by_place_ready")
        s_idx = sem("row_indices_ready")
        s_ri4 = sem("index_row_copied")
        s_turn = sem("pool_turns")
        s_g = [sem(f"gathered_{j}") for j in range(4)]
        s_sc = [sem(f"scattered_{j}") for j in range(4)]
        s_xtp = sem("x_transposed")
        s_xt = sem("x_rows_ready")
        s_up = sem("up_product")
        s_hb = sem("hidden_ready")
        s_htp = sem("hidden_transposed")
        s_hr = sem("hidden_rows_ready")
        s_dn = sem("down_product")
        s_y = sem("result_ready")
        s_xr = sem("residual_loaded")
        s_yr = [sem(f"results_loaded_{q}") for q in range(NT // SG)]
        s_o1 = sem("first_choice_added")
        s_o2 = sem("second_choice_scaled")
        s_o = sem("output_ready")
        s_out = sem("stored")

        def rep(a, n, many):
            return a.unsqueeze(1).to_broadcast([128, many, n])

        def cols(a, c, n, many):
            return a[:, bass.ds(c, many)].unsqueeze(2).to_broadcast([128, many, n])

        def at(i):
            return slice(i, i + 1) if isinstance(i, int) else bass.ds(i, 1)

        def need(eng, semaphore, count):
            if not (isinstance(count, int) and count <= 0):
                eng.wait_ge(semaphore, count)

        def stages(eng, quarter):
            def group(p, first):
                for u in units:
                    quarter(u, p, 0, p * T * UNITS + u, True, u < 3 and not first, not first)
                with eng.Fori(1, T - 1) as t:
                    for u in units:
                        quarter(u, p, t, (p * T + t) * UNITS + u, False, False, False)
                for u in units:
                    quarter(u, p, T - 1, (p * T + T - 1) * UNITS + u, False, u == 3, False)

            group(0, True)
            with eng.Fori(1, GROUPS) as p:
                group(p, False)
            for u in units:
                quarter(u, GROUPS, 0, GROUPS * T * UNITS + u, False, u < 3, True)

        def entering(i):
            return not (isinstance(i, int) and i >= GROUPS * T * UNITS)

        def running(i, lag):
            return not isinstance(i, int) or 0 <= i - lag < GROUPS * T * UNITS

        def behind(u, p, t, lag):
            v = (u - lag) % UNITS
            if u >= lag:
                return v, p, t
            return (v, p - 1, T - 1) if isinstance(t, int) and t == 0 else (v, p, t - 1)

        def i_round(i, j):
            return (i - j % 4) // 4 + 1 if isinstance(i, int) else rounds[0] * 2 + 1 + j // 4

        rounds = [None]

        def tiles(eng, step, experts=False):
            def body(r, i, last):
                word = [Experts(eng, r)] if experts else []
                for j in range(8):
                    step(i + j, j, 8 - j if last else 16, *word)

            with eng.Fori(0, MT // 8 - 1) as k:
                rounds[0] = k
                body(k, k * 8, False)
            body(MT // 8 - 1, MT - 8, True)

        class Experts:
            def __init__(self, eng, r):
                self.eng, self.r, self.words = eng, r, []
                self.read()

            def read(self):
                self.words.append(self.eng.value_load(te[0:1, at(self.r + len(self.words))], min_val=0, max_val=E ** 8 - 1))

            def __call__(self, n):
                return (self.words[n // 8] >> (3 * (n % 8))) & (E - 1)

        block = ctx.enter_context(nc.Block())

        from_one = [s_xs, s_xt, s_hb, s_hr, s_y]

        @block.sync
        def _(sp):
            for group in from_one:
                for one in group if isinstance(group, list) else [group]:
                    sp.sem_inc(one, 1)
            sp.sem_inc(s_ohp, 2)
            for dst, src in ((W[:, 0:COMMAND_COLS], wpack[:, 0:COMMAND_COLS]), (fs[:, :], fsT)):
                sp.dma_start(dst, src).then_inc(s_w, 16)

            def load_x(u, tok):
                sp.dma_start(xs[u][:, :], xT[:, bass.ds(tok, UT)]).then_inc(s_x[u], 16)

            def load_edges(u, g):
                sp.dma_start(ad[u][:, :, :], adj[bass.ds(g, UG), :, :].rearrange("g i j -> i g j")).then_inc(s_x[u], 16)

            def load_mask(u, tok):
                sp.dma_start(mk[u][:, :], mask[bass.ds(tok, UT)].partition_broadcast(128)).then_inc(s_x[u], 16)

            for u in units:
                load_x(u, u * UT)
                load_mask(u, u * UT)
                if u == 0:
                    for dst, src in ((bv[:, :], bvrow.partition_broadcast(128)), (bfc[:, :], bf_d), (idr[:, :], ident_d)):
                        sp.dma_start(dst, src).then_inc(s_w2, 16)
                load_edges(u, u * UG)
            with sp.Fori(1, GROUPS) as p:
                tok = [sp.snap((p * UNITS + u) * UT) for u in units]
                g = [sp.snap((p * UNITS + u) * UG) for u in units]
                used = [sp.snap(p * UNITS + u - 3) for u in units]
                masked = [sp.snap((p * T - 2) * UNITS + u + 1) for u in units]
                for u in units:
                    sp.wait_ge(s_cxp, used[u])
                    load_x(u, tok[u])
                    sp.wait_ge(s_eq, used[u])
                    load_edges(u, g[u])
                for u in units:
                    sp.wait_ge(s_mur, masked[u])
                    load_mask(u, tok[u])
            x_t = x.rearrange("(q g) n d -> q n g d", g=SG)
            out_t = out.rearrange("(q g) n d -> q n g d", g=SG)
            sp.wait_ge(s_grr, GROUPS * UNITS)
            sp.wait_ge(s_xm, GROUPS * UNITS)
            sp.wait_ge(s_pn, GROUPS * T * UNITS)
            for q in range(NT // SG):
                sp.dma_start(xres[q], x_t[q]).then_inc(s_xr, 16)
            for j in range(4):
                sp.wait_ge(s_sc[j], 16 * (MT // 4 + 1))
            for q in range(NT // SG):
                sp.dma_start(yin[q], y_s[:, q * SG:(q + 1) * SG, :, :]).then_inc(s_yr[q], 16)
            for q in range(NT // SG):
                sp.wait_ge(s_o, q + 1)
                sp.dma_start(out_t[q], xres[q]).then_inc(s_out, 16)
            sp.wait_ge(s_out, 16 * (NT // SG))

        @block.tensor
        def _(pe):
            def mm(o, l, r, start=True, stop=True, **k):
                return nc.tensor.matmul(o, l, r, start=start, stop=stop, **k)

            pe.wait_ge(s_w, 32)
            mm(PS[0][:, 0:B], w("qinT"), fs[:, :]).then_inc(s_pp, 1)
            pe.wait_ge(s_pv_, 1)
            for t in range(T):
                last = mm(PS[1][:, t * B:(t + 1) * B], w(f"qtT{t}"), qbase[:, :])
            last.then_inc(s_pp, 1)
            pe.wait_ge(s_pe_, 2)
            mm(PS[2][:, 0:TB], w("pkT"), cmd[:, :])
            mm(PS[2][:, TB:2 * TB], w("pvT"), cmd[:, :]).then_inc(s_pp, 1)
            pe.wait_ge(s_w2, 64)
            for c in range(3):
                mm(PS[6][:, c * TYPES:(c + 1) * TYPES], w(f"q{c}"), w("w1T", TYPES))
            mm(PS[6][:, 16:16 + TYPES], w("b_q", 1).to_broadcast([128, 128]), w("w1T", TYPES)).then_inc(s_pp, 1)
            pe.wait_ge(s_pv_, 2)
            kw = KW[:, :, :].rearrange("p a i -> p (a i)")
            mm(PS[3][:, :], w("k0"), kw).then_inc(s_pp, 1)
            mm(PS[7][:, :], w("b_k", 1).to_broadcast([128, 128]), kw).then_inc(s_pp, 1)
            for c in range(1, 3):
                mm(PS[3 + c][:, :], w(f"k{c}"), kw).then_inc(s_pp, 1)
            pe.wait_ge(s_pv_, 3)


            def local(u, p, i):
                k = p * UNITS + u
                pe.wait_ge(s_x[u], 48 * (p + 1))
                need(pe, s_vac, i)
                for b in range(UG):
                    o = ps_v[:, b * 256:b * 256 + D + CC]
                    xb = xs[u][:, b * N:(b + 1) * N]
                    mm(o[:, 0:D + TYPES], xb, v0q[:, :], stop=False, skip_group_check=True)
                    last = mm(o[:, D + TYPES:], xb, Kef[:, 0, bass.ds(k * UG + b, 1), :].rearrange("p b c -> p (b c)"),
                              start=False, skip_group_check=True)
                last.then_inc(s_lp, 1)

            def local_gate(u, p):
                k = p * UNITS + u
                need(pe, s_grr, k - 3)
                need(pe, s_cx, k)
                mm(ps_x[:, 0:UT], w("plT"), xs[u][:, :]).then_inc(s_plp, 1)

            def local_combined(u, p):
                pe.wait_ge(s_pl, p * UNITS + u + 1)
                mm(ps_x[:, 0:UT], w("cb0T"), xs[u][:, :]).then_inc(s_cxp, 1)

            def context(u, p, t, i, new):
                if new:
                    pe.wait_ge(s_xc0, p * UNITS + u + 1)
                else:
                    pe.wait_ge(s_mur, i - 3)
                need(pe, s_prod, i)
                mm(ps_pc[:, 0:UT], w("pcT"), xc[u][:, :]).then_inc(s_pc, 1)

            def values(u, p, i, new):
                pe.wait_ge(s_prod, i + 1)
                pe.wait_ge(s_wx, 3 * (i + 1))
                need(pe, s_vac, i)
                if new:
                    pe.wait_ge(s_lr, p * UNITS + u + 1)
                for b in range(UG):
                    o = ps_v[:, b * VW:(b + 1) * VW]
                    mm(o, xc[u][:, b * N:(b + 1) * N], wx[u][:, b, 0, :], stop=False)
                    last = mm(o, prod[u][:, b * N:(b + 1) * N], wx[u][:, b, 1, :], start=False)
                last.then_inc(s_vp, 1)

            def score_rows(u, i):
                pe.wait_ge(s_spl, i + 1)
                need(pe, s_mg, i - 2)
                need(pe, s_at, i)
                nc.tensor.transpose(ps_act, parts[u][:, :, :].rearrange("p b c -> p (b c)"), identb).then_inc(s_ap, 1)

            def edge_scores(v, pb, i, b):
                if b == 0:
                    pe.wait_ge(s_at, i + 1)
                    pe.wait_ge(s_eq, pb * UNITS + v + 1)
                need(pe, s_sm, UG * i + b - 1)
                o = ps_s[b]
                mm(o[:, :], acT[v][:, :], selA[:, b, :], stop=False)
                for r in range(TYPES):
                    mm(o[:, r * N:(r + 1) * N], selC[:, b, r, :], acT[v][:, :], start=False, stop=False)
                mm(o[:, :], negid, eqn[v][:, b, :, :].rearrange("p r j -> p (r j)"), start=False).then_inc(s_s, 1)

            def probs_T(v, i):
                need(pe, s_pt, i)
                pe.wait_ge(s_pn, i + 1)
                for b in range(UG):
                    last = nc.tensor.transpose(ps_pt[:, b * N:(b + 1) * N], pn[v][:, b, :], ident)
                last.then_inc(s_ptp, 1)

            def message(v, i):
                pe.wait_ge(s_pt, i + 1)
                need(pe, s_mg, i)
                pe.wait_ge(s_at, min(i + 3, GROUPS * T * UNITS) if isinstance(i, int) else i + 3)
                for b in range(UG):
                    last = mm(ps_msg[:, b * N:(b + 1) * N], vac[v][:, b, 0:D], pT[v][:, b, :])
                last.then_inc(s_mp, 1)

            def update_context(v, i):
                need(pe, s_mur, i)
                mm(ps_mu[:, 0:UT], w("mu0T"), xc[v][:, :], stop=False)

            def update_message(v, i):
                pe.wait_ge(s_mg, i + 1)
                mm(ps_mu[:, 0:UT], w("mu1T"), msg[v][:, :, :].rearrange("p b i -> p (b i)"), start=False).then_inc(s_mu, 1)

            def combine(v, f, started, i):
                pe.wait_ge(s_mur, i + 1)
                need(pe, s_grr, f)
                pe.wait_ge(s_cx, started)
                mm(ps_x[:, 0:UT], w("cb1T"), xctx[v][:, :]).then_inc(s_cb, 1)

            def gate_and_rows(v, f):
                pe.wait_ge(s_xm, f + 1)
                for b in range(UG):
                    mm(ps_x[:, b * E:(b + 1) * E], xm[v][:, b * N:(b + 1) * N], w("gateT", E))
                for b in range(UG):
                    last = nc.tensor.transpose(ps_x[:, (b + 1) * 128:(b + 2) * 128], xm[v][:, b * N:(b + 1) * N], ident)
                last.then_inc(s_gr, 1)

            def quarter(u, p, t, i, new, last, old):
                vb, pb, _ = behind(u, p, t, 1)
                vd, pd, _ = behind(u, p, t, 3)
                if running(i, 3):
                    probs_T(vd, i - 3)
                    update_context(vd, i - 3)
                if old:
                    gate_and_rows(u, (p - 1) * UNITS + u)
                if new:
                    local(u, p, i)
                if running(i, 1):
                    score_rows(vb, i - 1)
                if new:
                    local_gate(u, p)
                if entering(i):
                    context(u, p, t, i, new)
                if running(i, 3):
                    message(vd, i - 3)
                if running(i, 1):
                    edge_scores(vb, pb, i - 1, 0)
                if new:
                    local_combined(u, p)
                if entering(i):
                    values(u, p, i, new)
                if running(i, 3):
                    update_message(vd, i - 3)
                if running(i, 1):
                    edge_scores(vb, pb, i - 1, 1)
                if last:
                    combine(vd, pd * UNITS + vd, p * UNITS + u + 1 if new else (pd + 1) * UNITS, i - 3)
            stages(pe, quarter)

            pe.wait_ge(s_fw, 32)
            pe.wait_ge(s_sc[1], 16)
            pe.wait_ge(s_sel, 1)
            flat = selb[:, :, :].rearrange("p t e -> p (t e)")
            for h in range(2):
                last = mm(PS[0][:, h:h + 1], flat[:, h * 128:(h + 1) * 128], rc_one)
            last.then_inc(s_rp, 1)
            pe.wait_ge(s_cnt, 1)
            mm(PS[1][:, 0:NT * E], rc_tri, flat, stop=False)
            for h in range(2):
                mm(PS[1][:, 0:NT * E], cntb[:, h:h + 1].to_broadcast([128, 128]), rc_m[:, h, :], start=False, stop=h == 1)
            for h in range(2):
                last = mm(PS[2][:, 0:E], cntb[:, h:h + 1].to_broadcast([128, 128]), rc_t[:, h, :], start=h == 0, stop=h == 1)
            last.then_inc(s_rp, 1)
            slots = PS[3][:, 0:2 * MT]
            mm(slots, zero[:, 0:128], zero[:, :], stop=False, skip_group_check=True)
            with pe.Fori(0, NT * KTOP // (2 * OC)) as k:
                for h in range(2):
                    pe.wait_ge(s_oh, k * 2 + h + 1)
                    pe.wait_ge(s_oha, k * 2 + h + 1)
                    pe.wait_ge(s_ohg, k * 2 + h + 1)
                    for c in range(OC):
                        last = mm(slots, ohl[h][:, c, :], ohr[h][:, c, :, :].rearrange("p a m -> p (a m)"),
                                  start=False, stop=False, skip_group_check=True)
                    last.then_inc(s_ohp, 1)
            mm(slots, zero[:, 0:128], zero[:, :], start=False, skip_group_check=True).then_inc(s_rp, 1)

            def x_transpose(i, j):
                pe.wait_ge(s_g[j % 4], i_round(i, j) * 16)
                pe.wait_ge(s_xt, i + 1)
                nc.tensor.transpose(PS[6][:, 0:128], xg[j % 4][:, :], ident).then_inc(s_xtp, 1)

            def up(i, j, e):
                pe.wait_ge(s_xt, i + 2)
                need(pe, s_hb, i)
                mm(PS[j % 2][:, :], xt[j % 2][:, :], w1s[:, bass.ds(e, 1), :].rearrange("p e f -> p (e f)")).then_inc(s_up, 1)

            def h_transpose(i, j):
                pe.wait_ge(s_hb, i + 2)
                pe.wait_ge(s_hr, i + 1)
                for c in range(FC):
                    last = nc.tensor.transpose(PS[2 + j % 2][:, c * 128:(c + 1) * 128], hb[j % 2][:, c * 128:(c + 1) * 128], ident)
                last.then_inc(s_htp, 1)

            def down(i, j, e):
                pe.wait_ge(s_hr, i + 2)
                pe.wait_ge(s_y, i + 1)
                for c in range(FC):
                    last = mm(PS[4 + j % 2][:, 0:D], hT[j % 2][:, c * 128:(c + 1) * 128],
                              w2s[:, bass.ds(e, 1), c, :].rearrange("p e f -> p (e f)"), start=c == 0, stop=c == FC - 1)
                last.then_inc(s_dn, 1)

            
            pe.wait_ge(s_te, 1)
            pe.wait_ge(s_grr, GROUPS * UNITS)
            x_transpose(0, 0)
            x_transpose(1, 1)
            first = Experts(pe, 0)
            up(0, 0, first(0))
            up(1, 1, first(1))
            x_transpose(2, 2)
            h_transpose(0, 0)

            def step(i, j, left, expert):
                if left > 2:
                    up(i + 2, j + 2, expert(j + 2))
                if j == 5 and left > 8:
                    expert.read()
                if left > 3:
                    x_transpose(i + 3, j + 3)
                down(i, j, expert(j))
                if left > 1:
                    h_transpose(i + 1, j + 1)
            tiles(pe, step, experts=True)

        @block.scalar
        def _(act):
            def actv(o, i, f, **k):
                return nc.scalar.activation(o, i, f, **k)

            act.dma_start(W[:, COMMAND_COLS:], wpack[:, COMMAND_COLS:]).then_inc(s_w2, 16)
            act.wait_ge(s_warm, 1)
            actv(warm[:, :], warm[:, :], ACT.Exp)
            act.wait_ge(s_q, 2)
            actv(qb_e[:, :], qb_e[:, :], ACT.Exp).then_inc(s_pe_, 1)
            act.wait_ge(s_pp, 2)
            for t in range(T):
                last = actv(cmd[:, t * B:(t + 1) * B], PS[1][:, t * B:(t + 1) * B], ACT.Identity, bias=W[:, WOFF["b_qt"] + t:WOFF["b_qt"] + t + 1])
            last.then_inc(s_pe_, 1)
            act.wait_ge(s_x[UNITS - 1], 48)
            for dst, src in ((w1s[:, :, :], w1), (w2s[:, :, :, :], w2)):
                act.dma_start(dst, src).then_inc(s_fw, 16)
            act.wait_ge(s_pp, 8)
            actv(Kef[:, 2, :, :].rearrange("p b (t i) -> p b t i", t=T),
                 PS[5][:, :].rearrange("p (t b i) -> p b t i", t=T, b=B), ACT.Copy).then_inc(s_kc, 1)

            def quarter(u, p, t, i, new, last, old):
                vb, _, _ = behind(u, p, t, 1)
                vc, _, _ = behind(u, p, t, 2)
                vd, pd, td = behind(u, p, t, 3)
                if running(i, 3):
                    act.wait_ge(s_ptp, i - 2)
                    actv(pT[vd][:, :, :], ps_pt[:, 0:UT].rearrange("p (b i) -> p b i", b=UG), ACT.Copy).then_inc(s_pt, 1)
                if old:
                    f = (p - 1) * UNITS + u
                    act.wait_ge(s_gr, f + 1)
                    actv(lg[:, bass.ds(f * UG, UG), :], ps_x[:, 0:UG * E].rearrange("p (b e) -> p b e", b=UG), ACT.Copy)
                    act.wait_ge(s_xs[u % 2], 16 * ((p - 1) * 2 + u // 2) + 1)
                    actv(xrow[u % 2][:, :, :], ps_x[:, 128:128 + UT].rearrange("p (b d) -> p b d", b=UG), ACT.Copy).then_inc(s_grr, 1)
                if running(i, 1):
                    act.wait_ge(s_ap, i)
                    actv(acT[vb][:, :], ps_act, ACT.Copy).then_inc(s_at, 1)
                if new:
                    act.wait_ge(s_plp, p * UNITS + u + 1)
                    actv(pl[u][:, :], ps_x[:, 0:UT], ACT.Identity, bias=w("b_pl", 1)).then_inc(s_pl, 1)
                if running(i, 3):
                    act.wait_ge(s_mp, i - 2)
                    for b in range(UG):
                        one = actv(msg[vd][:, b, :], ps_msg[:, b * N:(b + 1) * N], ACT.Copy,
                                   scale=cv[:, at(td * B + (pd * UNITS + vd) * UG + b)])
                    one.then_inc(s_mg, 1)
                if running(i, 2):
                    act.wait_ge(s_lk, i - 1)
                    for b in range(UG):
                        actv(pr[vc][:, b, :], pr[vc][:, b, :], ACT.Exp, bias=nm[vc][:, b:b + 1],
                             accum_out=rs[vc][:, b:b + 1]).then_inc(s_ex, 1)
                if new:
                    act.wait_ge(s_cxp, p * UNITS + u + 1)
                    actv(cbx[u][:, :], ps_x[:, 0:UT], ACT.Identity, bias=w("b_cb", 1)).then_inc(s_cx, 1)
                if old:
                    act.wait_ge(s_grr, f + 1)
                    act.dma_start(xm_s[:, bass.ds(f * UG, UG), :], xrow[u % 2][:, :, :]).then_inc(s_xs[u % 2], 16)
                if last:
                    act.wait_ge(s_mu, i - 2)
                    actv(xctx[vd][:, :], ps_mu[:, 0:UT], ACT.Identity, bias=w("b_mu", 1)).then_inc(s_mur, 1)
            stages(act, quarter)
            act.wait_ge(s_gx, 1)
            actv(g1[:, :, :], g1[:, :, :], ACT.Exp).then_inc(s_exg, 1)

            with act.Fori(0, NT * KTOP // (2 * OC)) as k:
                for h in range(2):
                    act.wait_ge(s_ohh, k * 2 + h + 1)
                    actv(ohr[h][:, :, 0, :], ohh[h][:, :, :], ACT.Copy, scale=rf_place).then_inc(s_oha, 1)

            def x_out(i, j):
                act.wait_ge(s_xtp, i + 1)
                actv(xt[j % 2][:, :], PS[6][:, 0:128], ACT.Copy).then_inc(s_xt, 1)

            x_out(0, 0)
            x_out(1, 1)
            x_out(2, 2)

            def step(i, j, left):
                act.wait_ge(s_htp, i + 1)
                actv(hT[j % 2][:, :], PS[2 + j % 2][:, :], ACT.Relu).then_inc(s_hr, 1)
                if left > 3:
                    x_out(i + 3, j + 3)
            tiles(act, step)

            for q in range(NT // SG):
                act.wait_ge(s_yr[q], 16)
                for b in range(SG):
                    t = q * SG + b
                    last = actv(yin[q][:, b, 1, :], yin[q][:, b, 1, :], ACT.Copy, scale=gk[:, t:t + 1, 1])
                last.then_inc(s_o2, 1)

        @block.gpsimd
        def _(pool):
            g = nc.gpsimd
            pool.wait_ge(s_x[UNITS - 1], 48)
            for j, (dst, src) in enumerate(((rcf[:, :], rcf_d), (rcb[:, :], rcb_d),
                                            (b1s[:, :, :], b1.partition_broadcast(128)), (b2s[:, :, :], b2.partition_broadcast(128)))):
                g.dma_start(dst, src).then_inc(s_sc[j], 16)
            pool.wait_ge(s_pv_, 4)
            pool.wait_ge(s_kc, 1)

            def step_weights(u, p, t, i, new):
                need(pool, s_vp, i - 3)
                need(pool, s_vac, i - 3)
                if new:
                    pool.wait_ge(s_lr, p * UNITS + u + 1)
                pool.sem_inc(s_turn, 1)
                g.tensor_copy(loc[u][:, :, D + TYPES:].unsqueeze(2), locC[u][:, :, at(t), :]).then_inc(s_wx, 1)
                for c in range(2):
                    g.tensor_copy(wx[u][:, :, c, D + TYPES:],
                                  Kef[:, c + 1, bass.ds((p * UNITS + u) * UG, UG), bass.ds(t * TYPES, TYPES)]).then_inc(s_wx, 1)

            def quarter(u, p, t, i, new, last, old):
                vc, _, _ = behind(u, p, t, 2)
                if entering(i):
                    step_weights(u, p, t, i, new)
                if running(i, 2):
                    pool.wait_ge(s_ri, i - 1)
                    g.tensor_tensor(pn[vc][:, :, :], pr[vc][:, :, :], ri[vc][:, :].unsqueeze(2).to_broadcast([128, UG, N]),
                                    ALU.mult).then_inc(s_pn, 1)
            stages(pool, quarter)

            with pool.Fori(0, NT * KTOP // (2 * OC)) as k:
                for h in range(2):
                    q = k * 2 + h
                    pool.wait_ge(s_ohh, q + 1)
                    g.tensor_tensor(ohr[h][:, :, 1, :], ohh[h][:, :, :], cols(rb_num, q * OC, MT, OC), ALU.mult).then_inc(s_ohg, 1)

            def next_rows(r, h):
                g.tensor_copy(rows_c[h][:, :, :], rows[:, at(r), :, :].rearrange("p r a j -> p (r a) j")).then_inc(s_ri4, 1)
                pool.wait_ge(s_ri4, r + 1)
                pool.sem_inc(s_turn, 1)

            def gather(h, j):
                g.indirect_dma_start(xg[j][:, :], None, xm_d,
                                     bass.IndirectOffsetOnAxis(ap=rows_c[h][:, 1, j:j + 1], axis=0)).then_inc(s_g[j], 16)

            def scatter(i, h, j):
                pool.wait_ge(s_y, i + 2)
                pool.sem_inc(s_turn, 1)
                g.indirect_dma_start(y_d, bass.IndirectOffsetOnAxis(ap=rows_c[h][:, 0, j:j + 1], axis=0), yb[j][:, :], None,
                                     bounds_check=KTOP * TOK - 1, oob_is_err=False).then_inc(s_sc[j], 16)

            for j in range(2):
                pool.wait_ge(s_xs[j], 8 * GROUPS * UNITS + 1)
            pool.wait_ge(s_idx, 1)
            next_rows(0, 0)
            for j in range(4):
                gather(0, j)
            next_rows(1, 1)
            for j in range(4):
                pool.wait_ge(s_xtp, j + 1)
                pool.sem_inc(s_turn, 1)
                gather(1, j)

            def round4(r, h, more):
                next_rows(r, h)
                for j in range(4):
                    if more:
                        pool.wait_ge(s_xtp, (r - 1) * 4 + j + 1)
                        pool.sem_inc(s_turn, 1)
                        gather(h, j)
                    scatter((r - 2) * 4 + j, h, j)
            with pool.Fori(1, MT // 8) as k:
                round4(k * 2, 0, True)
                round4(k * 2 + 1, 1, True)
            round4(MT // 4, 0, False)
            round4(MT // 4 + 1, 1, False)

        @block.vector
        def _(dve):
            v = nc.vector

            v.memset(warm[:, :], 0.0).then_inc(s_warm, 1)
            for u in units:
                v.memset(parts[u][:, :, :], 0.0)
            dve.wait_ge(s_w, 32)
            dve.wait_ge(s_pp, 1)
            v.tensor_scalar(qb_r[:, :], PS[0][:, 0:B], w("b_qin", 1), 0.0, ALU.add, ALU.max).then_inc(s_q, 1)
            v.tensor_scalar(qb_e[:, :], PS[0][:, 0:B], w("b_qin", 1), 0.0, ALU.add, ALU.min).then_inc(s_q, 1)
            dve.wait_ge(s_pe_, 1)
            dve.wait_ge(s_q, 2)
            v.scalar_tensor_tensor(qbase[:, :], qb_e[:, :], -1.0, qb_r[:, :], ALU.add, ALU.add).then_inc(s_pv_, 1)
            dve.wait_ge(s_w2, 64)
            for u in units:
                for b in range(UG):
                    for c in range(2):
                        v.tensor_copy(wx[u][:, b, c, 0:D], w(f"v{c + 1}T"))
            v.tensor_copy(v0q[:, 0:D], w("v0T"))
            dve.wait_ge(s_pp, 3)
            v.tensor_scalar(ck[:, :], PS[2][:, 0:TB], w("b_pk", 1), None, ALU.add).then_inc(s_cvr, 1)
            dve.wait_ge(s_cvr, 1)
            for i in range(TYPES):
                last = v.tensor_scalar(KW[:, :, i], ck[:, :], W[:, WOFF["w2T"] + i:WOFF["w2T"] + i + 1], None, ALU.mult)
            last.then_inc(s_pv_, 1)
            v.tensor_scalar(cv[:, :], PS[2][:, TB:2 * TB], w("b_pv", 1), None, ALU.add).then_inc(s_cvr, 1)
            dve.wait_ge(s_pp, 4)
            v.tensor_copy(Q[:, :, :], PS[6][:, 0:3 * TYPES].rearrange("p (c i) -> p c i", c=3)).then_inc(s_cvr, 1)
            v.tensor_copy(bcst[:, 0:TYPES], PS[6][:, 16:16 + TYPES])
            dve.wait_ge(s_cvr, 3)
            v.tensor_copy(v0q[:, D:], Q[:, 0, :])
            for u in units:
                for b in range(UG):
                    v.tensor_copy(wx[u][:, b, :, D:D + TYPES], Q[:, 1:3, :])

            def key_vectors(c):
                return v.tensor_copy(Kef[:, c, :, :].rearrange("p b (t i) -> p b t i", t=T),
                                     PS[3 + c][:, :].rearrange("p (t b i) -> p b t i", t=T, b=B))

            dve.wait_ge(s_pp, 5)
            key_vectors(0)
            dve.wait_ge(s_pp, 6)
            v.tensor_copy(bcst[:, TYPES:].rearrange("p (b t i) -> p b t i", b=B, t=T),
                          PS[7][:, :].rearrange("p (t b i) -> p b t i", t=T, b=B)).then_inc(s_pv_, 1)
            dve.wait_ge(s_pp, 7)
            key_vectors(1).then_inc(s_pv_, 1)
            dve.wait_ge(s_pv_, 4)

            def start_unit(u, p, i):
                dve.wait_ge(s_x[u], 48 * (p + 1))
                need(dve, s_mu, i - 3)
                v.tensor_scalar(xc[u][:, :], mk[u][:, :], w("init", 1), None, ALU.mult).then_inc(s_xc0, 1)

            def edge_masks(u, i):
                need(dve, s_s, UG * (i - 3))
                for r in range(TYPES):
                    one = v.tensor_scalar(eqn[u][:, :, r, :], ad[u][:, :, :], r + 1, None, ALU.not_equal)
                one.then_inc(s_eq, 1)

            def local(u, p, i):
                k = p * UNITS + u
                dve.wait_ge(s_lp, k + 1)
                need(dve, s_wx, 3 * (i - 3))
                o = ps_v[:, :].rearrange("p (g c) -> p g c", g=UG)
                v.tensor_tensor(loc[u][:, :, 0:D], o[:, :, 0:D], bv[:, :].unsqueeze(1).to_broadcast([128, UG, D]), ALU.add)
                v.tensor_tensor(loc[u][:, :, D:D + TYPES], o[:, :, D:D + TYPES],
                                bcst[:, 0:TYPES].unsqueeze(1).to_broadcast([128, UG, TYPES]), ALU.add)
                v.tensor_tensor(locC[u][:, :, :, :].rearrange("p b t i -> p b (t i)"), o[:, :, D + TYPES:D + CC],
                                bcst[:, TYPES:].rearrange("p (b c) -> p b c", b=B)[:, bass.ds(k * UG, UG), :], ALU.add).then_inc(s_lr, 1)

            def edge_max(v_, i, b):
                dve.wait_ge(s_s, UG * i + b + 1)
                v.tensor_reduce(sc[v_][:, b, :], ps_s[b][:, :].rearrange("p (r j) -> p j r", r=TYPES),
                                AX.X, ALU.max).then_inc(s_sm, 1)

            def quarter(u, p, t, i, new, last, old):
                vb, _, _ = behind(u, p, t, 1)
                vc, _, _ = behind(u, p, t, 2)
                vd, pd, _ = behind(u, p, t, 3)
                if new:
                    start_unit(u, p, i)
                    local(u, p, i)
                if running(i, 2):
                    dve.wait_ge(s_sm, UG * (i - 1))
                    v.scalar_tensor_tensor(pr[vc][:, :, :], sc[vc][:, :, :], ALPHA, sc[vc][:, :, :], ALU.mult, ALU.max).then_inc(s_le, 1)
                if entering(i):
                    dve.wait_ge(s_pc, i + 1)
                    if new:
                        dve.wait_ge(s_pl, p * UNITS + u + 1)
                    v.scalar_tensor_tensor(prod[u][:, :], ps_pc[:, 0:UT], w("b_pc", 1), pl[u][:, :], ALU.add, ALU.mult).then_inc(s_prod, 1)
                if running(i, 2):
                    dve.wait_ge(s_le, i - 1)
                    v.tensor_reduce(nm[vc][:, :], pr[vc][:, :, :], AX.X, ALU.max, negate=True).then_inc(s_lk, 1)
                if running(i, 1):
                    edge_max(vb, i - 1, 0)
                if new:
                    edge_masks(u, i)
                if running(i, 2):
                    dve.wait_ge(s_ex, UG * (i - 1))
                    v.reciprocal(ri[vc][:, :], rs[vc][:, :]).then_inc(s_ri, 1)
                if entering(i):
                    dve.wait_ge(s_vp, i + 1)
                    v.tensor_tensor(vac[u][:, :, :], ps_v[:, 0:UG * VW].rearrange("p (g c) -> p g c", g=UG),
                                    loc[u][:, :, :], ALU.add).then_inc(s_vac, 1)
                    score = vac[u][:, :, D:]
                    dve.wait_ge(s_vac, i + 1)
                    v.tensor_copy(parts[u][:, 0:UG, 0:AC], score).then_inc(s_st, 1)
                if running(i, 3) and not last:
                    dve.wait_ge(s_mu, i - 2)
                    v.scalar_tensor_tensor(xc[vd][:, :], ps_mu[:, 0:UT], w("b_mu", 1), mk[vd][:, :], ALU.add, ALU.mult).then_inc(s_mur, 1)
                if entering(i):
                    dve.wait_ge(s_st, 3 * i + 1)
                    v.tensor_tensor(rest[u][:, :, :], score, parts[u][:, 0:UG, 0:AC], ALU.subtract).then_inc(s_st, 1)
                    dve.wait_ge(s_st, 3 * i + 2)
                    v.tensor_copy(parts[u][:, 0:UG, AC:2 * AC], rest[u][:, :, :]).then_inc(s_st, 1)
                    dve.wait_ge(s_st, 3 * i + 3)
                    v.tensor_tensor(parts[u][:, 0:UG, 2 * AC:3 * AC], rest[u][:, :, :], parts[u][:, 0:UG, AC:2 * AC], ALU.subtract).then_inc(s_spl, 1)
                if running(i, 1):
                    edge_max(vb, i - 1, 1)
                if last:
                    dve.wait_ge(s_cb, pd * UNITS + vd + 1)
                    v.tensor_tensor(xm[vd][:, :], ps_x[:, 0:UT], cbx[vd][:, :], ALU.add).then_inc(s_xm, 1)
            stages(dve, quarter)

            def bc(a):
                return a[:, :].unsqueeze(2).to_broadcast([128, NT, E])
            rk = rank[:, :].unsqueeze(1).to_broadcast([128, NT, E])
            steps = [0]

            def link(ins):
                ins.then_inc(s_gwork, 1)
                steps[0] += 1
                dve.wait_ge(s_gwork, steps[0])

            for j in range(4):
                dve.wait_ge(s_sc[j], 16)
            dve.wait_ge(s_grr, GROUPS * UNITS)
            link(v.tensor_reduce(gm[:, :], lg[:, :, :], AX.X, ALU.max))
            v.tensor_tensor(g1[:, :, :], lg[:, :, :], bc(gm), ALU.subtract).then_inc(s_gx, 1)
            dve.wait_ge(s_exg, 1)
            link(v.tensor_reduce(gm[:, :], g1[:, :, :], AX.X, ALU.add))
            link(v.reciprocal(gm[:, :], gm[:, :]))
            link(v.tensor_tensor(g1[:, :, :], g1[:, :, :], bc(gm), ALU.mult))

            def pick(prob, sel):
                link(v.tensor_reduce(gp[:, :], prob[:, :, :], AX.X, ALU.max))
                link(v.tensor_tensor(g3[:, :, :], prob[:, :, :], bc(gp), ALU.is_equal))
                link(v.tensor_tensor(g3[:, :, :], g3[:, :, :], rk, ALU.mult))
                link(v.tensor_reduce(gm[:, :], g3[:, :, :], AX.X, ALU.max))
                link(v.tensor_tensor(sel[:, :, :], g3[:, :, :], bc(gm), ALU.is_equal))

            pick(g1, sel1)
            link(v.tensor_copy(gk[:, :, 0], gp[:, :]))
            link(v.scalar_tensor_tensor(g2[:, :, :], sel1[:, :, :], -2.0, g1[:, :, :], ALU.mult, ALU.add))
            pick(g2, sel2)
            link(v.tensor_copy(gk[:, :, 1], gp[:, :]))
            v.tensor_tensor(selb[:, :, :], sel1[:, :, :], sel2[:, :, :], ALU.add).then_inc(s_sel, 1)

            dve.wait_ge(s_rp, 1)
            v.memset(zero[:, :], 0.0)
            v.tensor_copy(cntb[:, :], PS[0][:, 0:2]).then_inc(s_cnt, 1)
            dve.wait_ge(s_rp, 2)
            link(v.tensor_scalar(ti[:, :], PS[2][:, 0:E], 127.0, None, ALU.add))
            link(v.tensor_scalar(ti[:, :], ti[:, :], 7, None, ALU.arith_shift_right))
            link(v.tensor_copy(tf[:, :], ti[:, :]))
            link(v.tensor_tensor(t88[:, :, :], rf_tri[:, :, :], tf[:, :].unsqueeze(1).to_broadcast([128, E, E]), ALU.mult))
            link(v.tensor_reduce(tb[:, :], t88[:, :, :], AX.X, ALU.add))
            link(v.scalar_tensor_tensor(g2[:, :, :], tb[:, :].unsqueeze(1).to_broadcast([128, NT, E]), 128.0,
                                        PS[1][:, 0:NT * E].rearrange("p (t e) -> p t e", e=E), ALU.mult, ALU.add))
            for k, sel in enumerate((sel1, sel2)):
                link(v.tensor_tensor(g3[:, :, :], sel[:, :, :], g2[:, :, :], ALU.mult))
                link(v.tensor_reduce(pos[:, :, k], g3[:, :, :], AX.X, ALU.add))
            link(v.tensor_copy(posi[:, :, :], pos[:, :, :]))
            v.tensor_scalar(hii[:, :, :], posi[:, :, :], 7, None, ALU.arith_shift_right)
            link(v.tensor_scalar(loi[:, :, :], posi[:, :, :], 127, None, ALU.bitwise_and))
            v.tensor_copy(hib[:, :], hii[:, :, :].rearrange("p t k -> p (t k)"))
            link(v.tensor_copy(lob[:, :], loi[:, :, :].rearrange("p t k -> p (t k)")))

            with dve.Fori(0, NT * KTOP // (2 * OC)) as k:
                for h in range(2):
                    q = k * 2 + h
                    dve.wait_ge(s_ohp, q + 1)
                    v.tensor_tensor(ohh[h][:, :, :], cols(hib, q * OC, MT, OC), rep(rb_iota[:, 0:MT], MT, OC), ALU.is_equal).then_inc(s_ohh, 1)
                    v.tensor_tensor(ohl[h][:, :, :], cols(lob, q * OC, 128, OC), rep(rb_iota, 128, OC), ALU.is_equal).then_inc(s_oh, 1)
            dve.wait_ge(s_rp, 3)
            link(v.tensor_scalar(none[:, :], PS[3][:, MT:2 * MT], -1.0, None, ALU.add))
            link(v.scalar_tensor_tensor(slot[:, :], PS[3][:, 0:MT], float(NT * KTOP), none[:, :], ALU.mult, ALU.add))
            link(v.tensor_scalar(slot[:, :], slot[:, :], 0.0, None, ALU.max))
            link(v.tensor_scalar(none[:, :], none[:, :], -1.0, float(2 * KTOP * TOK), ALU.is_equal, ALU.mult))
            def by4(a):
                return a.rearrange("p (r j) -> p r j", j=4)
            v.memset(rows[:, 0:2, 0, :], 0)
            v.memset(rows[:, MT // 4:, 1, :], 0)
            v.tensor_tensor(rows[:, 2:, 0, :], by4(slot[:, :]), by4(none[:, :]), ALU.add)
            link(v.tensor_copy(rows[:, 0:MT // 4, 1, :], by4(slot[:, :])))
            v.tensor_scalar(rows[:, 0:MT // 4, 1, :], rows[:, 0:MT // 4, 1, :], 1, None, ALU.arith_shift_right).then_inc(s_idx, 1)

            link(v.tensor_tensor(tge[:, :, :], rf_iota[0:1, 0:MT].unsqueeze(2).to_broadcast([1, MT, E - 1]),
                                 tb[0:1, 1:E].unsqueeze(1).to_broadcast([1, MT, E - 1]), ALU.is_ge))
            link(v.tensor_reduce(tef[:, :], tge[:, :, :], AX.X, ALU.add))
            link(v.tensor_copy(tep[:, :], tef[:, 7::8]))
            for n in range(6, -1, -1):
                link(v.scalar_tensor_tensor(tep[:, :], tep[:, :], float(E), tef[:, n::8], ALU.mult, ALU.add))
            v.tensor_copy(te[:, :], tep[:, :]).then_inc(s_te, 1)

            def h_bias(i, j, e):
                dve.wait_ge(s_up, i + 1)
                v.tensor_tensor(hb[j % 2][:, :], PS[j % 2][:, :], b1s[:, bass.ds(e, 1), :].rearrange("p e f -> p (e f)"), ALU.add).then_inc(s_hb, 1)

            dve.wait_ge(s_te, 1)
            first = Experts(dve, 0)
            h_bias(0, 0, first(0))
            h_bias(1, 1, first(1))

            def step(i, j, left, expert):
                if j == 6 and left > 8:
                    expert.read()
                if left > 2:
                    h_bias(i + 2, j + 2, expert(j + 2))
                e = expert(j)
                dve.wait_ge(s_dn, i + 1)
                dve.wait_ge(s_sc[j % 4], i_round(i, j) * 16)
                v.tensor_tensor(yb[j % 4][:, :], PS[4 + j % 2][:, 0:D], b2s[:, bass.ds(e, 1), :].rearrange("p e f -> p (e f)"), ALU.add).then_inc(s_y, 1)
            tiles(dve, step, experts=True)

            dve.wait_ge(s_xr, 16 * (NT // SG))
            for q in range(NT // SG):
                dve.wait_ge(s_yr[q], 16)
                for b in range(SG):
                    t = q * SG + b
                    v.scalar_tensor_tensor(xres[q][:, b, :], yin[q][:, b, 0, :], gk[:, t:t + 1, 0], xres[q][:, b, :],
                                           ALU.mult, ALU.add).then_inc(s_o1, 1)
                dve.wait_ge(s_o1, (q + 1) * SG)
                dve.wait_ge(s_o2, q + 1)
                v.tensor_tensor(xres[q], xres[q], yin[q][:, :, 1, :], ALU.add).then_inc(s_o, 1)


def kernel(**inputs):
    import numpy as np
    import ml_dtypes
    import concourse.bacc as bacc
    from concourse.bass_utils import run_bass_kernel_spmd

    a = {k: np.asarray(v) for k, v in inputs.items()}
    c = {k[8:]: v for k, v in a.items() if k.startswith("L0_cond_")}
    f = {k[7:]: v for k, v in a.items() if k.startswith("L0_ffn_")}
    steps = a["fside_BxSxS_0"][:STEPS]
    wes = a["cond_2048"]
    cols = ([f["gate_w"].T, wes[:TYPES, :D].T, wes[:TYPES, D:].T, a["mask_BxS_ff0"][:STEPS].T]
            + [c[k].reshape(D, 1) for k in ("b_qin", "b_pl", "b_pc", "b_q", "b_k", "b_pk", "b_pv", "b_mu", "b_cb")]
            + [c["init_mem"].reshape(D, 1)]
            + [c["w_qin"].T] + [steps[t].T for t in range(STEPS)] + [c["w_pk"].T, c["w_pv"].T]
            + [c["w_k"], c["w_q"], c["w_pl"].T, c["w_pc"].T]
            + [c["w_v"][:, i * D:(i + 1) * D].T for i in range(3)]
            + [c["w_mu"][:, i * D:(i + 1) * D].T for i in range(2)]
            + [c["w_cb"][:, i * D:(i + 1) * D].T for i in range(2)])
    sel_a = np.zeros((4, 32, UG, TYPES, N), np.float32)
    sel_c = np.zeros((4, 32, UG, TYPES, N), np.float32)
    for b in range(UG):
        for part in range(3):
            for r in range(TYPES):
                sel_a[b, part * AC + r, b, r, :] = 1
                sel_c[b, part * AC + TYPES + r, b, r, :] = 1
    eye = np.eye(128, dtype=np.float32)
    consts = np.concatenate([eye, -BIG * eye, sel_a.reshape(128, -1), sel_c.reshape(128, -1)], 1).astype(ml_dtypes.bfloat16)
    place = np.arange(128)
    rcf = np.concatenate([np.tile(place, (128, 1)), place[:, None],
                          np.tile(np.tril(np.ones((E, E)), -1).reshape(1, -1), (128, 1))], 1).astype(np.float32)
    cell = np.arange(NT * E)
    same = cell[:, None] % E == cell[None, :] % E
    earlier = same & (cell[:, None] // E < cell[None, :] // E)
    rcb = np.concatenate([place[:, None] < place[None, :]] + [earlier[h * 128:(h + 1) * 128] for h in range(2)]
                         + [same[h * 128:(h + 1) * 128, :E] for h in range(2)] + [np.ones((128, 1)), np.tile(place, (128, 1)), np.tile(np.arange(NT * KTOP) + 1, (128, 1))], 1).astype(ml_dtypes.bfloat16)
    arrays = {
        "xT": a["x"].reshape(TOK, D).T, "x": a["x"], "mask": a["mask_BxS_ff1"].reshape(TOK), "adj": a["itok_BxSxS_0_4"],
        "fsT": a["fside_BxS_0"].T, "wpack": np.concatenate(cols, 1), "bvrow": c["b_v"],
        "w1": f["w1"].transpose(1, 0, 2), "b1": f["b1"],
        "w2": f["w2"].reshape(E, FC, 128, D).transpose(2, 0, 1, 3), "b2": f["b2"],
        "ident_d": np.concatenate([eye, np.tile(np.arange(E, 0, -1, dtype=np.float32), (128, 1))], 1), "bf_d": consts,
        "rcf_d": rcf, "rcb_d": rcb,
    }
    nc = bacc.Bacc("TRN2", target_bir_lowering=False, num_devices=1)
    args = {}
    for name, arr in list(arrays.items()):
        arrays[name] = arr = np.ascontiguousarray(arr)
        args[name] = nc.dram_tensor(name, arr.shape, mybir.dt.from_np(arr.dtype), kind="ExternalInput").ap()
    args["out"] = nc.dram_tensor("out", (B, N, D), mybir.dt.float32, kind="ExternalOutput").ap()
    build(nc, **args)
    return run_bass_kernel_spmd(nc, [arrays], core_ids=[0]).results[0]["out"]
```

```python
import concourse.bass as bass
from concourse import mybir
from contextlib import ExitStack

B, N, D = 32, 128, 128
TOK = B * N
STEPS = 4
TYPES = 4
E, F = 8, 512
FC = F // 128
UG = 2
UNITS = 4
GROUPS = B // (UG * UNITS)
UT = UG * N
SG = 4
NT = TOK // 128
KTOP = 2
MT = -(-(KTOP * TOK // 128 + E - 1) // 8) * 8
ALPHA = 0.2
BIG = 9000000000000000.0
AC = 2 * TYPES
VW = D + AC

WNAMES = (["qinT"] + [f"qtT{t}" for t in range(STEPS)] + ["pkT", "pvT"] + ["k0", "k1", "k2", "q0", "q1", "q2"]
          + ["plT", "pcT", "v0T", "v1T", "v2T", "mu0T", "mu1T", "cb0T", "cb1T", "mu0", "mu1"])
SMALL = [("gateT", E), ("w1T", TYPES), ("w2T", TYPES), ("b_qt", STEPS)] + [
    (b, 1) for b in ("b_qin", "b_pl", "b_pc", "b_q", "b_k", "b_pk", "b_pv", "b_mu", "b_cb", "init")]
WOFF = {}
WCOLS = 0
for _n, _w in SMALL + [(w, D) for w in WNAMES]:
    WOFF[_n] = WCOLS
    WCOLS += _w
COMMAND_COLS = WOFF["k0"]


def build(nc, xT, x, mask, adj, fsT, wpack, bvrow, w1, b1, w2, b2, ident_d, bf_d, rcf_d, rcb_d, out):
    fp32, bf16, i32 = mybir.dt.float32, mybir.dt.bfloat16, mybir.dt.int32
    ALU = mybir.AluOpType
    ACT = mybir.ActivationFunctionType
    AX = mybir.AxisListType
    TB = STEPS * B

    ctx = ExitStack()
    with ctx:
        def sb(name, shape, dt=fp32):
            return ctx.enter_context(nc.sbuf_tensor(name, shape, dt))

        def sem(name):
            return ctx.enter_context(nc.semaphore(name))

        W = sb("W", [128, WCOLS])

        def w(name, width=D):
            return W[:, WOFF[name]:WOFF[name] + width]

        bv = sb("bv", [128, D])
        idr = sb("idr", [128, 128 + E])
        ident = idr[:, 0:128]
        rank = idr[:, 128:]
        BFC = 256 + UG * TYPES * 128 * 2
        bfc = sb("bfc", [128, BFC], bf16)
        identb = bfc[:, 0:128]
        negid = bfc[:, 128:256]
        selA = bfc[:, 256:256 + UG * TYPES * 128].rearrange("p (b c) -> p b c", b=UG)
        selC = bfc[:, 256 + UG * TYPES * 128:].rearrange("p (b r i) -> p b r i", b=UG, r=TYPES)
        Q = sb("Q", [128, 3, TYPES])
        v0q = sb("v0q", [128, D + TYPES])
        cmT = sb("cmT", [128, 2, D])
        pc0 = sb("pc0", [128, 1])
        b_cm = sb("b_cm", [128, 1])
        fs = sb("fs", [128, B])
        warm = sb("warm", [128, 1])
        qb_e = sb("qb_e", [128, B])
        qb_r = sb("qb_r", [128, B])
        qbase = sb("qbase", [128, B])
        cmd = sb("cmd", [128, TB])
        ck = sb("ck", [128, TB])
        cv = sb("cv", [128, TB])
        KW = sb("KW", [128, TB, TYPES])
        Kef = sb("Kef", [128, 3, B, STEPS * TYPES])
        bcst = sb("bcst", [128, TYPES + B * STEPS * TYPES])
        units = range(UNITS)
        xs = [sb(f"xs{u}", [128, UT]) for u in units]
        mk = [sb(f"mk{u}", [128, UT]) for u in units]
        ad = [sb(f"ad{u}", [128, UG, N], i32) for u in units]
        eqn = [sb(f"eqn{u}", [128, UG, TYPES, N], bf16) for u in units]
        pl = [sb(f"pl{u}", [128, UT]) for u in units]
        cbx = [sb(f"cbx{u}", [128, UT]) for u in units]
        xc = [sb(f"xc{u}", [128, UT]) for u in units]
        prod = [sb(f"prod{u}", [128, UT]) for u in units]
        wx = [sb(f"wx{u}", [128, UG, 2, VW]) for u in units]
        loc = [sb(f"loc{u}", [128, UG, VW]) for u in units]
        locC = [sb(f"locC{u}", [128, UG, STEPS, TYPES]) for u in units]
        vac = [sb(f"vac{u}", [128, UG, VW]) for u in units]
        rest = [sb(f"rest{u}", [128, UG, AC]) for u in units]
        parts = [sb(f"parts{u}", [128, 4, 32], bf16) for u in units]
        acT = [sb(f"acT{u}", [128, 128], bf16) for u in units]
        sc = [sb(f"sc{u}", [128, UG, N]) for u in units]
        nm = [sb(f"nm{u}", [128, UG]) for u in units]
        rs = [sb(f"rs{u}", [128, UG]) for u in units]
        ri = [sb(f"ri{u}", [128, UG]) for u in units]
        pr = [sb(f"pr{u}", [128, UG, N]) for u in units]
        pn = [sb(f"pn{u}", [128, UG, N]) for u in units]
        pT = [sb(f"pT{u}", [128, UG, N]) for u in units]
        msg = [sb(f"msg{u}", [128, UG, N]) for u in units]
        xm = [sb(f"xm{u}", [128, UT]) for u in units]
        lg = sb("lg", [128, NT, E])
        g1 = sb("g1", [128, NT, E])
        g2 = sb("g2", [128, NT, E])
        g3 = sb("g3", [128, NT, E])
        sel1 = sb("sel1", [128, NT, E])
        sel2 = sb("sel2", [128, NT, E])
        selb = sb("selb", [128, NT, E], bf16)
        gm = sb("gm", [128, NT])
        gk = sb("gk", [128, NT, KTOP])
        cntb = sb("cntb", [128, 2], bf16)
        ti = sb("ti", [128, E], i32)
        tf = sb("tf", [128, E])
        t88 = sb("t88", [128, E, E])
        tb = sb("tb", [128, E])
        tge = sb("tge", [1, MT, E - 1])
        tef = sb("tef", [1, MT])
        tep = sb("tep", [1, MT // 8])
        te = sb("te", [1, MT // 8], i32)
        pos = sb("pos", [128, NT, KTOP])
        posi = sb("posi", [128, NT, KTOP], i32)
        hii = sb("hii", [128, NT, KTOP], i32)
        loi = sb("loi", [128, NT, KTOP], i32)
        OC = 8
        lob = sb("lob", [128, NT * KTOP], bf16)
        hib = sb("hib", [128, NT * KTOP], bf16)
        ohl = [sb(f"ohl{j}", [128, OC, 128], bf16) for j in range(2)]
        ohh = [sb(f"ohh{j}", [128, OC, MT], bf16) for j in range(2)]
        ohr = [sb(f"ohr{j}", [128, OC, 2, MT], bf16) for j in range(2)]
        zero = sb("zero", [128, 2 * MT], bf16)
        slot = sb("slot", [128, MT])
        none = sb("none", [128, MT])
        rows = sb("rows", [128, MT // 4 + 2, 2, 4], i32)
        rows_c = [sb(f"rows_c{h}", [128, 2, 4], i32) for h in range(2)]
        rcf = sb("rcf", [128, 128 + 1 + E * E])
        rf_iota = rcf[:, 0:128]
        rf_place = rcf[:, 128:129]
        rf_tri = rcf[:, 129:].rearrange("p (a b) -> p a b", a=E)
        RB = 128 + 2 * NT * E + 2 * E + 1
        rcb = sb("rcb", [128, RB + 128 + NT * KTOP], bf16)
        rb_iota = rcb[:, RB:RB + 128]
        rb_num = rcb[:, RB + 128:]
        rc_tri = rcb[:, 0:128]
        rc_m = rcb[:, 128:128 + 2 * NT * E].rearrange("p (h c) -> p h c", h=2)
        rc_t = rcb[:, 128 + 2 * NT * E:128 + 2 * NT * E + 2 * E].rearrange("p (h c) -> p h c", h=2)
        rc_one = rcb[:, RB - 1:RB]
        xrow = [sb(f"xrow{i}", [128, UG, D]) for i in range(2)]
        w1s = sb("w1s", [128, E, F])
        w2s = sb("w2s", [128, E, FC, D])
        b1s = sb("b1s", [128, E * FC])
        b2s = sb("b2s", [128, E, D])
        xg = [sb(f"xg{j}", [128, D]) for j in range(4)]
        xt = [sb(f"xt{j}", [128, 128]) for j in range(2)]
        w1t = [sb(f"w1t{j}", [128, F]) for j in range(2)]
        hT = [sb(f"hT{j}", [128, F]) for j in range(2)]
        yb = [sb(f"yb{j}", [128, D]) for j in range(8)]
        KF = Kef[:, :, :, :].rearrange("p c b i -> p (c b i)")
        XW = SG * D
        xres = [(W[:, q * XW:(q + 1) * XW] if q < 5 else KF[:, (q - 5) * XW:(q - 4) * XW]).rearrange("p (b d) -> p b d", b=SG)
                for q in range(NT // SG)]
        YW = SG * KTOP * D
        w1f = w1s[:, :, :].rearrange("p e f -> p (e f)")
        w2f = w2s[:, :, :, :].rearrange("p e c d -> p (e c d)")
        yin = [(w1f[:, q * YW:(q + 1) * YW] if q < 4 else w2f[:, (q - 4) * YW:(q - 3) * YW]).rearrange(
            "p (b k d) -> p b k d", b=SG, k=KTOP) for q in range(NT // SG)]
        xm_s = nc.dram_tensor("xm_rows", [128, NT, D], fp32, kind="Internal").ap()
        xm_d = xm_s.rearrange("p t d -> (p t) d")
        y_s = nc.dram_tensor("expert_rows", [128, NT, KTOP, D], fp32, kind="Internal").ap()
        y_d = y_s.rearrange("p t k d -> (p t k) d")

        PS = [ctx.enter_context(nc.psum_tensor(f"ps{i}", [128, 512], fp32)) for i in range(8)]
        ps_pc, ps_v, ps_s, ps_pt, ps_msg, ps_mu, ps_x = PS[0], PS[1], PS[2:4], PS[4], PS[5], PS[6], PS[7]
        ps_act = ps_x[:, :].bitcast(bf16)[:, 0:128]
        CC = TYPES * (1 + STEPS)

        s_w = sem("command_weights_loaded")
        s_w2 = sem("other_weights_loaded")
        s_const = sem("constants_loaded")
        s_fw = sem("expert_weights_loaded")
        s_pp = sem("setup_product")
        s_setup_act = sem("setup_scalar_done")
        s_setup_vec = sem("setup_vector_done")
        s_kc = sem("last_key_vectors_ready")
        s_warm = sem("exp_argument_ready")
        s_x = [sem(f"unit_loaded_{u}") for u in units]
        s_lp = sem("local_product")
        s_lr = sem("local_ready")
        s_plp = sem("gate_projection")
        s_pl = sem("gate_projection_ready")
        s_cxp = sem("local_combined_product")
        s_cx = sem("local_combined_ready")
        s_eq = sem("edge_masks_ready")
        s_xc0 = sem("first_context_ready")
        s_pc = sem("context_product")
        s_pr0 = sem("first_projection_ready")
        s_prod = sem("gated_product_ready")
        s_wx = sem("value_weights_ready")
        s_vp = sem("value_product")
        s_vac = sem("value_ready")
        s_st = sem("score_split_steps")
        s_spl = sem("score_parts_ready")
        s_ap = sem("score_transposed")
        s_at = sem("score_rows_ready")
        s_s = sem("edge_scores")
        s_sm = sem("edge_scores_read")
        s_le = sem("leaky_done")
        s_lk = sem("logits_ready")
        s_ex = sem("exp_done")
        s_ri = sem("row_sum_inverse")
        s_pn = sem("probs_ready")
        s_ptp = sem("probs_transposed")
        s_pt = sem("probs_T_ready")
        s_mp = sem("message_product")
        s_mg = sem("message_ready")
        s_mu = sem("update_product")
        s_mur = sem("context_updated")
        s_gr = sem("gate_and_row_product")
        s_grr = sem("gate_and_row_read")
        s_q = sem("query_base_steps")
        s_setup_step = sem("setup_steps")
        s_exg = sem("gate_exp_done")
        s_gx = sem("gate_max_subtracted")

        T = STEPS

        s_xs = [sem(f"rows_stored_{j}") for j in range(2)]
        s_gwork = sem("gate_steps")
        s_sel = sem("choices_ready")
        s_rp = sem("routing_product")
        s_cnt = sem("tile_counts_ready")
        s_te = sem("tile_experts_ready")
        s_oh = sem("one_hots_ready")
        s_ohp = sem("one_hots_read")
        s_ohh = sem("tile_one_hots_ready")
        s_ohg = sem("tile_one_hots_by_column_ready")
        s_oha = sem("tile_one_hots_by_place_ready")
        s_row = sem("index_row_copied")
        s_turn = sem("pool_turns")
        s_g = [sem(f"gathered_{j}") for j in range(4)]
        s_sc = [sem(f"scattered_{j}") for j in range(8)]
        s_xtp = sem("x_transposed")
        s_xt = sem("x_rows_ready")
        s_up = sem("up_product")
        s_w1t = sem("first_weights_ready")
        s_hr = sem("hidden_rows_ready")
        s_dn = sem("down_product")
        s_y = sem("result_ready")
        s_xr = sem("residual_loaded")
        s_yr = [sem(f"results_loaded_{q}") for q in range(NT // SG)]
        s_o1 = sem("first_choice_added")
        s_o2 = sem("second_choice_scaled")
        s_o = sem("output_ready")
        s_out = sem("stored")

        def rep(a, n, many):
            return a.unsqueeze(1).to_broadcast([128, many, n])

        def cols(a, c, n, many):
            return a[:, bass.ds(c, many)].unsqueeze(2).to_broadcast([128, many, n])

        def at(i):
            return slice(i, i + 1) if isinstance(i, int) else bass.ds(i, 1)

        def need(eng, semaphore, count):
            if not (isinstance(count, int) and count <= 0):
                eng.wait_ge(semaphore, count)

        def stages(eng, quarter):
            def group(p, first):
                for u in units:
                    quarter(u, p, 0, p * T * UNITS + u, True, u < 3 and not first, not first)
                with eng.Fori(1, T - 1) as t:
                    for u in units:
                        quarter(u, p, t, (p * T + t) * UNITS + u, False, False, False)
                for u in units:
                    quarter(u, p, T - 1, (p * T + T - 1) * UNITS + u, False, u == 3, False)

            group(0, True)
            with eng.Fori(1, GROUPS) as p:
                group(p, False)
            for u in units:
                quarter(u, GROUPS, 0, GROUPS * T * UNITS + u, False, u < 3, True)

        def entering(i):
            return not (isinstance(i, int) and i >= GROUPS * T * UNITS)

        def running(i, lag):
            return not isinstance(i, int) or 0 <= i - lag < GROUPS * T * UNITS

        def behind(u, p, t, lag):
            v = (u - lag) % UNITS
            if u >= lag:
                return v, p, t
            return (v, p - 1, T - 1) if isinstance(t, int) and t == 0 else (v, p, t - 1)

        def i_round(i, j):
            return (i - j % 4) // 4 + 1 if isinstance(i, int) else rounds[0] * 2 + 1 + j // 4

        rounds = [None]

        def tiles(eng, step, experts=False):
            def body(r, i, last):
                word = [Experts(eng, r)] if experts else []
                for j in range(8):
                    step(i + j, j, 8 - j if last else 16, *word)

            with eng.Fori(0, MT // 8 - 1) as k:
                rounds[0] = k
                body(k, k * 8, False)
            body(MT // 8 - 1, MT - 8, True)

        class Experts:
            def __init__(self, eng, r):
                self.eng, self.r, self.words = eng, r, []

            def read(self):
                self.words.append(self.eng.value_load(te[0:1, at(self.r + len(self.words))], min_val=0, max_val=E ** 8 - 1))

            def __call__(self, n):
                return (self.words[n // 8] >> (3 * (n % 8))) & (E - 1)

        block = ctx.enter_context(nc.Block())

        from_one = [s_xs, s_xt, s_hr]

        @block.sync
        def _(sp):
            for group in from_one:
                for one in group if isinstance(group, list) else [group]:
                    sp.sem_inc(one, 1)
            sp.sem_inc(s_dn, 2)
            sp.sem_inc(s_y, 2)
            sp.sem_inc(s_ohp, 2)
            for dst, src in ((W[:, 0:COMMAND_COLS], wpack[:, 0:COMMAND_COLS]), (fs[:, :], fsT)):
                sp.dma_start(dst, src).then_inc(s_w, 16)

            def load_x(u, tok):
                sp.dma_start(xs[u][:, :], xT[:, bass.ds(tok, UT)]).then_inc(s_x[u], 16)

            def load_edges(u, g):
                sp.dma_start(ad[u][:, :, :], adj[bass.ds(g, UG), :, :].rearrange("g i j -> i g j")).then_inc(s_x[u], 16)

            def load_mask(u, tok):
                sp.dma_start(mk[u][:, :], mask[bass.ds(tok, UT)].partition_broadcast(128)).then_inc(s_x[u], 16)

            sp.dma_start(W[:, COMMAND_COLS:], wpack[:, COMMAND_COLS:]).then_inc(s_w2, 16)
            for u in units:
                load_x(u, u * UT)
                load_mask(u, u * UT)
                if u == 0:
                    for dst, src in ((bv[:, :], bvrow.partition_broadcast(128)), (bfc[:, :], bf_d), (idr[:, :], ident_d)):
                        sp.dma_start(dst, src).then_inc(s_const, 16)
                load_edges(u, u * UG)
            with sp.Fori(1, GROUPS) as p:
                tok = [sp.snap((p * UNITS + u) * UT) for u in units]
                g = [sp.snap((p * UNITS + u) * UG) for u in units]
                used = [sp.snap(p * UNITS + u - 3) for u in units]
                masked = [sp.snap((p * T - 2) * UNITS + u + 1) for u in units]
                for u in units:
                    sp.wait_ge(s_cxp, used[u])
                    load_x(u, tok[u])
                    sp.wait_ge(s_eq, used[u])
                    load_edges(u, g[u])
                for u in units:
                    sp.wait_ge(s_mur, masked[u])
                    load_mask(u, tok[u])
            x_t = x.rearrange("(q g) n d -> q n g d", g=SG)
            out_t = out.rearrange("(q g) n d -> q n g d", g=SG)
            sp.wait_ge(s_grr, GROUPS * UNITS)
            sp.wait_ge(s_mur, GROUPS * T * UNITS)
            sp.wait_ge(s_pn, GROUPS * T * UNITS)
            for q in range(NT // SG):
                sp.dma_start(xres[q], x_t[q]).then_inc(s_xr, 16)
            for j in range(8):
                sp.wait_ge(s_sc[j], 16 * (MT // 8 + 1))
            for q in range(NT // SG):
                sp.dma_start(yin[q], y_s[:, q * SG:(q + 1) * SG, :, :]).then_inc(s_yr[q], 16)
            for q in range(NT // SG):
                sp.wait_ge(s_o, q + 1)
                sp.dma_start(out_t[q], xres[q]).then_inc(s_out, 16)
            sp.wait_ge(s_out, 16 * (NT // SG))

        @block.tensor
        def _(pe):
            def mm(o, l, r, start=True, stop=True, **k):
                return nc.tensor.matmul(o, l, r, start=start, stop=stop, **k)

            pe.wait_ge(s_w, 32)
            mm(PS[0][:, 0:B], w("qinT"), fs[:, :]).then_inc(s_pp, 1)
            pe.wait_ge(s_setup_vec, 1)
            for t in range(T):
                last = mm(PS[1][:, t * B:(t + 1) * B], w(f"qtT{t}"), qbase[:, :])
            last.then_inc(s_pp, 1)
            pe.wait_ge(s_setup_act, 2)
            mm(PS[2][:, 0:TB], w("pkT"), cmd[:, :])
            mm(PS[2][:, TB:2 * TB], w("pvT"), cmd[:, :]).then_inc(s_pp, 1)
            pe.wait_ge(s_w2, 16)
            for c in range(3):
                mm(PS[6][:, c * TYPES:(c + 1) * TYPES], w(f"q{c}"), w("w1T", TYPES))
            mm(PS[6][:, 16:16 + TYPES], w("b_q", 1).to_broadcast([128, 128]), w("w1T", TYPES)).then_inc(s_pp, 1)
            pe.wait_ge(s_setup_vec, 2)
            kw = KW[:, :, :].rearrange("p a i -> p (a i)")
            mm(PS[3][:, :], w("k0"), kw).then_inc(s_pp, 1)
            mm(PS[7][:, :], w("b_k", 1).to_broadcast([128, 128]), kw).then_inc(s_pp, 1)
            pe.wait_ge(s_setup_step, 4)
            mm(PS[6][:, 24:25], w("pcT"), w("init", 1))
            mm(PS[6][:, 25:26], w("cb1T"), w("b_mu", 1))
            for c in range(2):
                last = mm(PS[6][:, (c + 1) * D:(c + 2) * D], w(f"mu{c}"), w("cb1T"))
            last.then_inc(s_pp, 1)
            for c in range(1, 3):
                mm(PS[3 + c][:, :], w(f"k{c}"), kw).then_inc(s_pp, 1)
            pe.wait_ge(s_const, 48)
            pe.wait_ge(s_setup_vec, 3)

            def local(u, p, i):
                k = p * UNITS + u
                pe.wait_ge(s_x[u], 48 * (p + 1))
                need(pe, s_vac, i)
                for b in range(UG):
                    o = ps_v[:, b * 256:b * 256 + D + CC]
                    xb = xs[u][:, b * N:(b + 1) * N]
                    mm(o[:, 0:D + TYPES], xb, v0q[:, :], stop=False, skip_group_check=True)
                    last = mm(o[:, D + TYPES:], xb, Kef[:, 0, bass.ds(k * UG + b, 1), :].rearrange("p b c -> p (b c)"),
                              start=False, skip_group_check=True)
                last.then_inc(s_lp, 1)

            def local_gate(u, p, i):
                k = p * UNITS + u
                need(pe, s_at, i)
                need(pe, s_grr, k - 3)
                need(pe, s_cx, k)
                mm(ps_x[:, 0:UT], w("plT"), xs[u][:, :]).then_inc(s_plp, 1)

            def local_combined(u, p):
                pe.wait_ge(s_pl, p * UNITS + u + 1)
                mm(ps_x[:, 0:UT], w("cb0T"), xs[u][:, :]).then_inc(s_cxp, 1)

            def context(u, i):
                pe.wait_ge(s_mur, i - 3)
                need(pe, s_prod, i)
                mm(ps_pc[:, 0:UT], w("pcT"), xc[u][:, :]).then_inc(s_pc, 1)

            def values(u, p, i, new):
                pe.wait_ge(s_prod, i + 1)
                pe.wait_ge(s_wx, 3 * (i + 1))
                need(pe, s_vac, i)
                if new:
                    pe.wait_ge(s_xc0, p * UNITS + u + 1)
                    pe.wait_ge(s_lr, p * UNITS + u + 1)
                for b in range(UG):
                    o = ps_v[:, b * VW:(b + 1) * VW]
                    mm(o, xc[u][:, b * N:(b + 1) * N], wx[u][:, b, 0, :], stop=False)
                    last = mm(o, prod[u][:, b * N:(b + 1) * N], wx[u][:, b, 1, :], start=False)
                last.then_inc(s_vp, 1)

            def score_rows(u, i, started, ended):
                pe.wait_ge(s_spl, i + 1)
                need(pe, s_at, i)
                need(pe, s_cx, started)
                if ended is not None:
                    pe.wait_ge(s_grr, ended)
                nc.tensor.transpose(ps_act, parts[u][:, :, :].rearrange("p b c -> p (b c)"), identb).then_inc(s_ap, 1)

            def edge_scores(v, pb, i, b):
                if b == 0:
                    pe.wait_ge(s_at, i + 1)
                    pe.wait_ge(s_eq, pb * UNITS + v + 1)
                need(pe, s_sm, UG * i + b - 1)
                o = ps_s[b]
                mm(o[:, :], acT[v][:, :], selA[:, b, :], stop=False)
                for r in range(TYPES):
                    mm(o[:, r * N:(r + 1) * N], selC[:, b, r, :], acT[v][:, :], start=False, stop=False)
                mm(o[:, :], negid, eqn[v][:, b, :, :].rearrange("p r j -> p (r j)"), start=False).then_inc(s_s, 1)

            def probs_T(v, i):
                need(pe, s_pt, i)
                pe.wait_ge(s_pn, i + 1)
                for b in range(UG):
                    last = nc.tensor.transpose(ps_pt[:, b * N:(b + 1) * N], pn[v][:, b, :], ident)
                last.then_inc(s_ptp, 1)

            def message(v, i):
                pe.wait_ge(s_pt, i + 1)
                need(pe, s_mg, i)
                for b in range(UG):
                    last = mm(ps_msg[:, b * N:(b + 1) * N], vac[v][:, b, 0:D], pT[v][:, b, :])
                last.then_inc(s_mp, 1)

            def update_context(v, i, last):
                need(pe, s_mur, i)
                mm(ps_mu[:, 0:UT], cmT[:, 0, :] if last else w("mu0T"), xc[v][:, :], stop=False)

            def update_message(v, i, last):
                pe.wait_ge(s_mg, i + 1)
                mm(ps_mu[:, 0:UT], cmT[:, 1, :] if last else w("mu1T"), msg[v][:, :, :].rearrange("p b i -> p (b i)"),
                   start=False).then_inc(s_mu, 1)

            def gate_and_rows(v, f, i):
                pe.wait_ge(s_mur, i + 1)
                pe.wait_ge(s_cx, min(f + UNITS, GROUPS * UNITS) if isinstance(f, int) else f + UNITS)
                for b in range(UG):
                    mm(ps_x[:, b * E:(b + 1) * E], xm[v][:, b * N:(b + 1) * N], w("gateT", E))
                for b in range(UG):
                    last = nc.tensor.transpose(ps_x[:, (b + 1) * 128:(b + 2) * 128], xm[v][:, b * N:(b + 1) * N], ident)
                last.then_inc(s_gr, 1)

            def quarter(u, p, t, i, new, last, old):
                vb, pb, _ = behind(u, p, t, 1)
                vd, pd, _ = behind(u, p, t, 3)
                if running(i, 3):
                    probs_T(vd, i - 3)
                if old:
                    gate_and_rows(u, (p - 1) * UNITS + u, i - UNITS)
                if new:
                    local(u, p, i)
                if entering(i) and not new:
                    context(u, i)
                if running(i, 1):
                    score_rows(vb, i - 1, p * UNITS + u if isinstance(t, int) and t == 0 else (p + 1) * UNITS,
                               (p - 1) * UNITS + u + 1 if old else None)
                if running(i, 3):
                    update_context(vd, i - 3, last)
                if new:
                    local_gate(u, p, i)
                if running(i, 3):
                    message(vd, i - 3)
                if running(i, 1):
                    edge_scores(vb, pb, i - 1, 0)
                if new:
                    local_combined(u, p)
                if entering(i):
                    values(u, p, i, new)
                if running(i, 3):
                    update_message(vd, i - 3, last)
                if running(i, 1):
                    edge_scores(vb, pb, i - 1, 1)
            stages(pe, quarter)

            pe.wait_ge(s_fw, 32)
            pe.wait_ge(s_sc[2], 16)
            pe.wait_ge(s_sel, 1)
            flat = selb[:, :, :].rearrange("p t e -> p (t e)")
            for h in range(2):
                last = mm(PS[0][:, h:h + 1], flat[:, h * 128:(h + 1) * 128], rc_one)
            last.then_inc(s_rp, 1)
            pe.wait_ge(s_cnt, 1)
            mm(PS[1][:, 0:NT * E], rc_tri, flat, stop=False)
            for h in range(2):
                mm(PS[1][:, 0:NT * E], cntb[:, h:h + 1].to_broadcast([128, 128]), rc_m[:, h, :], start=False, stop=h == 1)
            for h in range(2):
                last = mm(PS[2][:, 0:E], cntb[:, h:h + 1].to_broadcast([128, 128]), rc_t[:, h, :], start=h == 0, stop=h == 1)
            last.then_inc(s_rp, 1)
            slots = PS[3][:, 0:2 * MT]
            mm(slots, zero[:, 0:128], zero[:, :], stop=False, skip_group_check=True)
            with pe.Fori(0, NT * KTOP // (2 * OC)) as k:
                for h in range(2):
                    pe.wait_ge(s_oh, k * 2 + h + 1)
                    pe.wait_ge(s_oha, k * 2 + h + 1)
                    pe.wait_ge(s_ohg, k * 2 + h + 1)
                    for c in range(OC):
                        last = mm(slots, ohl[h][:, c, :], ohr[h][:, c, :, :].rearrange("p a m -> p (a m)"),
                                  start=False, stop=False, skip_group_check=True)
                    last.then_inc(s_ohp, 1)
            mm(slots, zero[:, 0:128], zero[:, :], start=False, skip_group_check=True).then_inc(s_rp, 1)

            def x_transpose(i, j):
                pe.wait_ge(s_g[j % 4], i_round(i, j) * 16)
                pe.wait_ge(s_xt, i + 1)
                nc.tensor.transpose(PS[6][:, 0:128], xg[j % 4][:, :], ident).then_inc(s_xtp, 1)

            def up(i, j):
                pe.wait_ge(s_xt, i + 2)
                need(pe, s_hr, i)
                pe.wait_ge(s_w1t, i + 1)
                for c in range(FC):
                    last = mm(PS[j % 2][:, c * 128:(c + 1) * 128], w1t[j % 2][:, c * 128:(c + 1) * 128], xt[j % 2][:, :])
                last.then_inc(s_up, 1)

            def down(i, j, e):
                pe.wait_ge(s_hr, i + 2)
                pe.wait_ge(s_y, i + 1)
                for c in range(FC):
                    last = mm(PS[4 + j % 2][:, 0:D], hT[j % 2][:, c * 128:(c + 1) * 128],
                              w2s[:, bass.ds(e, 1), c, :].rearrange("p e f -> p (e f)"), start=c == 0, stop=c == FC - 1)
                last.then_inc(s_dn, 1)

            pe.wait_ge(s_te, 1)
            pe.wait_ge(s_grr, GROUPS * UNITS)
            x_transpose(0, 0)
            x_transpose(1, 1)
            up(0, 0)
            up(1, 1)
            x_transpose(2, 2)

            def step(i, j, left, expert):
                if left > 2:
                    up(i + 2, j + 2)
                if left > 3:
                    x_transpose(i + 3, j + 3)
                if j == 0:
                    expert.read()
                down(i, j, expert(j))
            tiles(pe, step, experts=True)

        @block.scalar
        def _(act):
            def actv(o, i, f, **k):
                return nc.scalar.activation(o, i, f, **k)

            act.wait_ge(s_warm, 1)
            actv(warm[:, :], warm[:, :], ACT.Exp)
            act.wait_ge(s_q, 2)
            actv(qb_e[:, :], qb_e[:, :], ACT.Exp).then_inc(s_setup_act, 1)
            act.wait_ge(s_pp, 2)
            for t in range(T):
                last = actv(cmd[:, t * B:(t + 1) * B], PS[1][:, t * B:(t + 1) * B], ACT.Identity, bias=W[:, WOFF["b_qt"] + t:WOFF["b_qt"] + t + 1])
            last.then_inc(s_setup_act, 1)
            act.wait_ge(s_x[UNITS - 1], 48)
            for dst, src in ((w1s[:, :, :], w1), (w2s[:, :, :, :], w2)):
                act.dma_start(dst, src).then_inc(s_fw, 16)
            act.wait_ge(s_pp, 9)
            actv(Kef[:, 2, :, :].rearrange("p b (t i) -> p b t i", t=T),
                 PS[5][:, :].rearrange("p (t b i) -> p b t i", t=T, b=B), ACT.Copy).then_inc(s_kc, 1)

            def quarter(u, p, t, i, new, last, old):
                vb, _, _ = behind(u, p, t, 1)
                vc, _, _ = behind(u, p, t, 2)
                vd, pd, td = behind(u, p, t, 3)
                if running(i, 3):
                    act.wait_ge(s_ptp, i - 2)
                    actv(pT[vd][:, :, :], ps_pt[:, 0:UT].rearrange("p (b i) -> p b i", b=UG), ACT.Copy).then_inc(s_pt, 1)
                if old:
                    f = (p - 1) * UNITS + u
                    act.wait_ge(s_gr, f + 1)
                    actv(lg[:, bass.ds(f * UG, UG), :], ps_x[:, 0:UG * E].rearrange("p (b e) -> p b e", b=UG), ACT.Copy)
                    act.wait_ge(s_xs[u % 2], 16 * ((p - 1) * 2 + u // 2) + 1)
                    actv(xrow[u % 2][:, :, :], ps_x[:, 128:128 + UT].rearrange("p (b d) -> p b d", b=UG), ACT.Copy).then_inc(s_grr, 1)
                if running(i, 1):
                    act.wait_ge(s_ap, i)
                    actv(acT[vb][:, :], ps_act, ACT.Copy).then_inc(s_at, 1)
                if new:
                    act.wait_ge(s_plp, p * UNITS + u + 1)
                    actv(pl[u][:, :], ps_x[:, 0:UT], ACT.Identity, bias=w("b_pl", 1)).then_inc(s_pl, 1)
                if running(i, 3):
                    act.wait_ge(s_mp, i - 2)
                    for b in range(UG):
                        one = actv(msg[vd][:, b, :], ps_msg[:, b * N:(b + 1) * N], ACT.Copy,
                                   scale=cv[:, at(td * B + (pd * UNITS + vd) * UG + b)])
                    one.then_inc(s_mg, 1)
                if running(i, 2):
                    act.wait_ge(s_lk, i - 1)
                    for b in range(UG):
                        actv(pr[vc][:, b, :], pr[vc][:, b, :], ACT.Exp, bias=nm[vc][:, b:b + 1],
                             accum_out=rs[vc][:, b:b + 1]).then_inc(s_ex, 1)
                if new:
                    act.wait_ge(s_cxp, p * UNITS + u + 1)
                    actv(cbx[u][:, :], ps_x[:, 0:UT], ACT.Identity, bias=b_cm[:, :]).then_inc(s_cx, 1)
                if old:
                    act.wait_ge(s_grr, f + 1)
                    act.dma_start(xm_s[:, bass.ds(f * UG, UG), :], xrow[u % 2][:, :, :]).then_inc(s_xs[u % 2], 16)
            stages(act, quarter)
            act.wait_ge(s_gx, 1)
            actv(g1[:, :, :], g1[:, :, :], ACT.Exp).then_inc(s_exg, 1)

            with act.Fori(0, NT * KTOP // (2 * OC)) as k:
                for h in range(2):
                    act.wait_ge(s_ohh, k * 2 + h + 1)
                    actv(ohr[h][:, :, 0, :], ohh[h][:, :, :], ACT.Copy, scale=rf_place).then_inc(s_oha, 1)

            def x_out(i, j):
                act.wait_ge(s_xtp, i + 1)
                actv(xt[j % 2][:, :], PS[6][:, 0:128], ACT.Copy).then_inc(s_xt, 1)

            def hidden(i, j, e):
                act.wait_ge(s_up, i + 1)
                act.wait_ge(s_dn, i + 1)
                for c in range(FC):
                    last = actv(hT[j % 2][:, c * 128:(c + 1) * 128], PS[j % 2][:, c * 128:(c + 1) * 128], ACT.Relu,
                                bias=b1s[:, bass.ds(e * FC + c, 1)])
                last.then_inc(s_hr, 1)

            act.wait_ge(s_te, 1)
            act.wait_ge(s_sc[4], 16)
            act.wait_ge(s_sc[5], 16)
            first = Experts(act, 0)
            first.read()
            x_out(0, 0)
            x_out(1, 1)
            hidden(0, 0, first(0))
            x_out(2, 2)
            hidden(1, 1, first(1))

            def step(i, j, left, expert):
                if left > 3:
                    x_out(i + 3, j + 3)
                if j == 0 or j == 5 and left > 8:
                    expert.read()
                if left > 2:
                    hidden(i + 2, j + 2, expert(j + 2))
            tiles(act, step, experts=True)

            for q in range(NT // SG):
                act.wait_ge(s_yr[q], 16)
                for b in range(SG):
                    t = q * SG + b
                    last = actv(yin[q][:, b, 1, :], yin[q][:, b, 1, :], ACT.Copy, scale=gk[:, t:t + 1, 1])
                last.then_inc(s_o2, 1)

        @block.gpsimd
        def _(pool):
            g = nc.gpsimd
            pool.wait_ge(s_x[UNITS - 1], 48)
            h = E // 2
            for j, (dst, src) in enumerate((
                    (rcf[:, 0:128], rcf_d[:, 0:128]), (rcf[:, 128:], rcf_d[:, 128:]),
                    (rcb[:, 0:RB], rcb_d[:, 0:RB]), (rcb[:, RB:], rcb_d[:, RB:]),
                    (b1s[:, 0:h * FC], b1[:, 0:h * FC]), (b1s[:, h * FC:], b1[:, h * FC:]),
                    (b2s[:, 0:h, :], b2[0:h, :].partition_broadcast(128)), (b2s[:, h:, :], b2[h:, :].partition_broadcast(128)))):
                g.dma_start(dst, src).then_inc(s_sc[j], 16)
            pool.wait_ge(s_setup_vec, 4)
            pool.wait_ge(s_kc, 1)

            def step_weights(u, p, t, i, new):
                need(pool, s_vp, i - 3)
                need(pool, s_vac, i - 3)
                if new:
                    pool.wait_ge(s_lr, p * UNITS + u + 1)
                pool.sem_inc(s_turn, 1)
                g.tensor_copy(loc[u][:, :, D + TYPES:].unsqueeze(2), locC[u][:, :, at(t), :]).then_inc(s_wx, 1)
                for c in range(2):
                    g.tensor_copy(wx[u][:, :, c, D + TYPES:],
                                  Kef[:, c + 1, bass.ds((p * UNITS + u) * UG, UG), bass.ds(t * TYPES, TYPES)]).then_inc(s_wx, 1)

            def quarter(u, p, t, i, new, last, old):
                vc, _, _ = behind(u, p, t, 2)
                if entering(i):
                    step_weights(u, p, t, i, new)
                if running(i, 2):
                    pool.wait_ge(s_ri, i - 1)
                    g.tensor_tensor(pn[vc][:, :, :], pr[vc][:, :, :], ri[vc][:, :].unsqueeze(2).to_broadcast([128, UG, N]),
                                    ALU.mult).then_inc(s_pn, 1)
            stages(pool, quarter)

            with pool.Fori(0, NT * KTOP // (2 * OC)) as k:
                for h in range(2):
                    q = k * 2 + h
                    pool.wait_ge(s_ohh, q + 1)
                    g.tensor_tensor(ohr[h][:, :, 1, :], ohh[h][:, :, :], cols(rb_num, q * OC, MT, OC), ALU.mult).then_inc(s_ohg, 1)

            def next_rows(r):
                pool.wait_ge(s_row, r + 1)
                pool.sem_inc(s_turn, 1)

            def gather(h, j):
                g.indirect_dma_start(xg[j][:, :], None, xm_d,
                                     bass.IndirectOffsetOnAxis(ap=rows_c[h][:, 1, j:j + 1], axis=0)).then_inc(s_g[j], 16)

            def scatter(i, h, j):
                pool.wait_ge(s_y, i + 3)
                pool.sem_inc(s_turn, 1)
                g.indirect_dma_start(y_d, bass.IndirectOffsetOnAxis(ap=rows_c[h][:, 0, j:j + 1], axis=0), yb[h * 4 + j][:, :], None,
                                     bounds_check=KTOP * TOK - 1, oob_is_err=False).then_inc(s_sc[h * 4 + j], 16)

            for j in range(2):
                pool.wait_ge(s_xs[j], 8 * GROUPS * UNITS + 1)
            next_rows(0)
            for j in range(4):
                gather(0, j)
            next_rows(1)
            for j in range(4):
                pool.wait_ge(s_xtp, j + 1)
                pool.sem_inc(s_turn, 1)
                gather(1, j)

            def round4(r, h, more):
                next_rows(r)
                for j in range(4):
                    if more:
                        pool.wait_ge(s_xtp, (r - 1) * 4 + j + 1)
                        pool.sem_inc(s_turn, 1)
                        gather(h, j)
                    scatter((r - 2) * 4 + j, h, j)
            with pool.Fori(1, MT // 8) as k:
                round4(k * 2, 0, True)
                round4(k * 2 + 1, 1, True)
            round4(MT // 4, 0, False)
            round4(MT // 4 + 1, 1, False)

        @block.vector
        def _(dve):
            v = nc.vector

            v.memset(warm[:, :], 0.0).then_inc(s_warm, 1)
            for u in units:
                v.memset(parts[u][:, :, :], 0.0)
            dve.wait_ge(s_w, 32)
            dve.wait_ge(s_pp, 1)
            v.tensor_scalar(qb_r[:, :], PS[0][:, 0:B], w("b_qin", 1), 0.0, ALU.add, ALU.max).then_inc(s_q, 1)
            v.tensor_scalar(qb_e[:, :], PS[0][:, 0:B], w("b_qin", 1), 0.0, ALU.add, ALU.min).then_inc(s_q, 1)
            dve.wait_ge(s_setup_act, 1)
            dve.wait_ge(s_q, 2)
            v.scalar_tensor_tensor(qbase[:, :], qb_e[:, :], -1.0, qb_r[:, :], ALU.add, ALU.add).then_inc(s_setup_vec, 1)
            dve.wait_ge(s_w2, 16)
            for u in units:
                for b in range(UG):
                    for c in range(2):
                        v.tensor_copy(wx[u][:, b, c, 0:D], w(f"v{c + 1}T"))
            v.tensor_copy(v0q[:, 0:D], w("v0T"))
            dve.wait_ge(s_pp, 3)
            v.tensor_scalar(ck[:, :], PS[2][:, 0:TB], w("b_pk", 1), None, ALU.add).then_inc(s_setup_step, 1)
            dve.wait_ge(s_setup_step, 1)
            for i in range(TYPES):
                last = v.tensor_scalar(KW[:, :, i], ck[:, :], W[:, WOFF["w2T"] + i:WOFF["w2T"] + i + 1], None, ALU.mult)
            last.then_inc(s_setup_vec, 1)
            v.tensor_scalar(cv[:, :], PS[2][:, TB:2 * TB], w("b_pv", 1), None, ALU.add).then_inc(s_setup_step, 1)
            dve.wait_ge(s_pp, 4)
            v.tensor_copy(Q[:, :, :], PS[6][:, 0:3 * TYPES].rearrange("p (c i) -> p c i", c=3)).then_inc(s_setup_step, 1)
            v.tensor_copy(bcst[:, 0:TYPES], PS[6][:, 16:16 + TYPES]).then_inc(s_setup_step, 1)
            dve.wait_ge(s_setup_step, 3)
            v.tensor_copy(v0q[:, D:], Q[:, 0, :])
            for u in units:
                for b in range(UG):
                    v.tensor_copy(wx[u][:, b, :, D:D + TYPES], Q[:, 1:3, :])

            def key_vectors(c):
                return v.tensor_copy(Kef[:, c, :, :].rearrange("p b (t i) -> p b t i", t=T),
                                     PS[3 + c][:, :].rearrange("p (t b i) -> p b t i", t=T, b=B))

            dve.wait_ge(s_pp, 5)
            key_vectors(0)
            dve.wait_ge(s_pp, 6)
            v.tensor_copy(bcst[:, TYPES:].rearrange("p (b t i) -> p b t i", b=B, t=T),
                          PS[7][:, :].rearrange("p (t b i) -> p b t i", t=T, b=B))
            dve.wait_ge(s_pp, 7)
            v.tensor_copy(pc0[:, :], PS[6][:, 24:25])
            v.tensor_scalar(b_cm[:, :], PS[6][:, 25:26], w("b_cb", 1), None, ALU.add)
            v.tensor_copy(cmT[:, :, :], PS[6][:, D:3 * D].rearrange("p (c d) -> p c d", c=2)).then_inc(s_setup_vec, 1)
            dve.wait_ge(s_const, 48)
            dve.wait_ge(s_pp, 8)
            key_vectors(1).then_inc(s_setup_vec, 1)
            dve.wait_ge(s_setup_vec, 4)

            def start_unit(u, p, i):
                dve.wait_ge(s_x[u], 48 * (p + 1))
                need(dve, s_mu, i - 3)
                v.tensor_scalar(xc[u][:, :], mk[u][:, :], w("init", 1), None, ALU.mult).then_inc(s_xc0, 1)

            def edge_mask(u, i, r):
                if r == 0:
                    need(dve, s_s, UG * (i - 3))
                one = v.tensor_scalar(eqn[u][:, :, r, :], ad[u][:, :, :], r + 1, None, ALU.not_equal)
                if r == TYPES - 1:
                    one.then_inc(s_eq, 1)

            def local(u, p, i):
                k = p * UNITS + u
                dve.wait_ge(s_lp, k + 1)
                need(dve, s_wx, 3 * (i - 3))
                o = ps_v[:, :].rearrange("p (g c) -> p g c", g=UG)
                v.tensor_tensor(loc[u][:, :, 0:D], o[:, :, 0:D], bv[:, :].unsqueeze(1).to_broadcast([128, UG, D]), ALU.add)
                v.tensor_tensor(loc[u][:, :, D:D + TYPES], o[:, :, D:D + TYPES],
                                bcst[:, 0:TYPES].unsqueeze(1).to_broadcast([128, UG, TYPES]), ALU.add)
                v.tensor_tensor(locC[u][:, :, :, :].rearrange("p b t i -> p b (t i)"), o[:, :, D + TYPES:D + CC],
                                bcst[:, TYPES:].rearrange("p (b c) -> p b c", b=B)[:, bass.ds(k * UG, UG), :], ALU.add).then_inc(s_lr, 1)

            def edge_max(v_, i, b):
                dve.wait_ge(s_s, UG * i + b + 1)
                v.tensor_reduce(sc[v_][:, b, :], ps_s[b][:, :].rearrange("p (r j) -> p j r", r=TYPES),
                                AX.X, ALU.max).then_inc(s_sm, 1)

            def quarter(u, p, t, i, new, last, old):
                vb, _, _ = behind(u, p, t, 1)
                vc, _, _ = behind(u, p, t, 2)
                vd, pd, _ = behind(u, p, t, 3)
                if new:
                    start_unit(u, p, i)
                    local(u, p, i)
                if running(i, 2):
                    dve.wait_ge(s_sm, UG * (i - 1))
                    v.scalar_tensor_tensor(pr[vc][:, :, :], sc[vc][:, :, :], ALPHA, sc[vc][:, :, :], ALU.mult, ALU.max).then_inc(s_le, 1)
                if new:
                    v.tensor_scalar(prod[u][:, :], mk[u][:, :], pc0[:, :], w("b_pc", 1), ALU.mult, ALU.add).then_inc(s_pr0, 1)
                    dve.wait_ge(s_pr0, p * UNITS + u + 1)
                    dve.wait_ge(s_pl, p * UNITS + u + 1)
                    v.tensor_tensor(prod[u][:, :], prod[u][:, :], pl[u][:, :], ALU.mult).then_inc(s_prod, 1)
                elif entering(i):
                    dve.wait_ge(s_pc, (p * (T - 1) + t - 1) * UNITS + u + 1)
                    v.scalar_tensor_tensor(prod[u][:, :], ps_pc[:, 0:UT], w("b_pc", 1), pl[u][:, :], ALU.add, ALU.mult).then_inc(s_prod, 1)
                if running(i, 2):
                    dve.wait_ge(s_le, i - 1)
                    v.tensor_reduce(nm[vc][:, :], pr[vc][:, :, :], AX.X, ALU.max, negate=True).then_inc(s_lk, 1)
                if running(i, 1):
                    edge_max(vb, i - 1, 0)
                if running(i, 2):
                    dve.wait_ge(s_ex, UG * (i - 1))
                    v.reciprocal(ri[vc][:, :], rs[vc][:, :]).then_inc(s_ri, 1)
                if entering(i):
                    dve.wait_ge(s_vp, i + 1)
                    v.tensor_tensor(vac[u][:, :, :], ps_v[:, 0:UG * VW].rearrange("p (g c) -> p g c", g=UG),
                                    loc[u][:, :, :], ALU.add).then_inc(s_vac, 1)
                    score = vac[u][:, :, D:]
                    if new:
                        edge_mask(u, i, 0)
                    dve.wait_ge(s_vac, i + 1)
                    v.tensor_copy(parts[u][:, 0:UG, 0:AC], score).then_inc(s_st, 1)
                if last:
                    dve.wait_ge(s_mu, i - 2)
                    dve.wait_ge(s_cx, pd * UNITS + vd + 1)
                    v.tensor_tensor(xm[vd][:, :], ps_mu[:, 0:UT], cbx[vd][:, :], ALU.add).then_inc(s_mur, 1)
                elif running(i, 3):
                    dve.wait_ge(s_mu, i - 2)
                    v.scalar_tensor_tensor(xc[vd][:, :], ps_mu[:, 0:UT], w("b_mu", 1), mk[vd][:, :], ALU.add, ALU.mult).then_inc(s_mur, 1)
                if entering(i):
                    if new:
                        edge_mask(u, i, 1)
                    dve.wait_ge(s_st, 3 * i + 1)
                    v.tensor_tensor(rest[u][:, :, :], score, parts[u][:, 0:UG, 0:AC], ALU.subtract).then_inc(s_st, 1)
                    if new:
                        edge_mask(u, i, 2)
                    dve.wait_ge(s_st, 3 * i + 2)
                    v.tensor_copy(parts[u][:, 0:UG, AC:2 * AC], rest[u][:, :, :]).then_inc(s_st, 1)
                    if new:
                        edge_mask(u, i, 3)
                    dve.wait_ge(s_st, 3 * i + 3)
                    v.tensor_tensor(parts[u][:, 0:UG, 2 * AC:3 * AC], rest[u][:, :, :], parts[u][:, 0:UG, AC:2 * AC], ALU.subtract).then_inc(s_spl, 1)
                if running(i, 1):
                    edge_max(vb, i - 1, 1)
            stages(dve, quarter)

            def bc(a):
                return a[:, :].unsqueeze(2).to_broadcast([128, NT, E])
            rk = rank[:, :].unsqueeze(1).to_broadcast([128, NT, E])
            steps = [0]

            def link(ins):
                ins.then_inc(s_gwork, 1)
                steps[0] += 1
                dve.wait_ge(s_gwork, steps[0])

            for j in range(8):
                dve.wait_ge(s_sc[j], 16)
            dve.wait_ge(s_grr, GROUPS * UNITS)
            link(v.tensor_reduce(gm[:, :], lg[:, :, :], AX.X, ALU.max))
            v.tensor_tensor(g1[:, :, :], lg[:, :, :], bc(gm), ALU.subtract).then_inc(s_gx, 1)
            dve.wait_ge(s_exg, 1)
            link(v.tensor_reduce(gm[:, :], g1[:, :, :], AX.X, ALU.add))
            link(v.reciprocal(gm[:, :], gm[:, :]))
            link(v.tensor_tensor(g1[:, :, :], g1[:, :, :], bc(gm), ALU.mult))

            def pick(prob, sel, k):
                link(v.tensor_reduce(gk[:, :, k], prob[:, :, :], AX.X, ALU.max))
                link(v.tensor_tensor(g3[:, :, :], prob[:, :, :], gk[:, :, k:k + 1].to_broadcast([128, NT, E]), ALU.is_equal))
                link(v.tensor_tensor(g3[:, :, :], g3[:, :, :], rk, ALU.mult))
                link(v.tensor_reduce(gm[:, :], g3[:, :, :], AX.X, ALU.max))
                link(v.tensor_tensor(sel[:, :, :], g3[:, :, :], bc(gm), ALU.is_equal))

            pick(g1, sel1, 0)
            link(v.scalar_tensor_tensor(g2[:, :, :], sel1[:, :, :], -2.0, g1[:, :, :], ALU.mult, ALU.add))
            pick(g2, sel2, 1)
            v.tensor_tensor(selb[:, :, :], sel1[:, :, :], sel2[:, :, :], ALU.add).then_inc(s_sel, 1)

            dve.wait_ge(s_rp, 1)
            v.memset(zero[:, :], 0.0)
            v.tensor_copy(cntb[:, :], PS[0][:, 0:2]).then_inc(s_cnt, 1)
            dve.wait_ge(s_rp, 2)
            link(v.tensor_scalar(ti[:, :], PS[2][:, 0:E], 127.0, None, ALU.add))
            link(v.tensor_scalar(ti[:, :], ti[:, :], 7, None, ALU.arith_shift_right))
            link(v.tensor_copy(tf[:, :], ti[:, :]))
            link(v.tensor_tensor(t88[:, :, :], rf_tri[:, :, :], tf[:, :].unsqueeze(1).to_broadcast([128, E, E]), ALU.mult))
            link(v.tensor_reduce(tb[:, :], t88[:, :, :], AX.X, ALU.add))
            link(v.scalar_tensor_tensor(g2[:, :, :], tb[:, :].unsqueeze(1).to_broadcast([128, NT, E]), 128.0,
                                        PS[1][:, 0:NT * E].rearrange("p (t e) -> p t e", e=E), ALU.mult, ALU.add))
            for k, sel in enumerate((sel1, sel2)):
                link(v.tensor_tensor(g3[:, :, :], sel[:, :, :], g2[:, :, :], ALU.mult))
                link(v.tensor_reduce(pos[:, :, k], g3[:, :, :], AX.X, ALU.add))
            link(v.tensor_copy(posi[:, :, :], pos[:, :, :]))
            v.tensor_scalar(hii[:, :, :], posi[:, :, :], 7, None, ALU.arith_shift_right)
            link(v.tensor_scalar(loi[:, :, :], posi[:, :, :], 127, None, ALU.bitwise_and))
            v.tensor_copy(hib[:, :], hii[:, :, :].rearrange("p t k -> p (t k)"))
            link(v.tensor_copy(lob[:, :], loi[:, :, :].rearrange("p t k -> p (t k)")))

            with dve.Fori(0, NT * KTOP // (2 * OC)) as k:
                for h in range(2):
                    q = k * 2 + h
                    dve.wait_ge(s_ohp, q + 1)
                    v.tensor_tensor(ohh[h][:, :, :], cols(hib, q * OC, MT, OC), rep(rb_iota[:, 0:MT], MT, OC), ALU.is_equal).then_inc(s_ohh, 1)
                    v.tensor_tensor(ohl[h][:, :, :], cols(lob, q * OC, 128, OC), rep(rb_iota, 128, OC), ALU.is_equal).then_inc(s_oh, 1)
            dve.wait_ge(s_rp, 3)
            link(v.tensor_scalar(none[:, :], PS[3][:, MT:2 * MT], -1.0, None, ALU.add))
            link(v.scalar_tensor_tensor(slot[:, :], PS[3][:, 0:MT], float(NT * KTOP), none[:, :], ALU.mult, ALU.add))
            link(v.tensor_scalar(slot[:, :], slot[:, :], 0.0, None, ALU.max))
            link(v.tensor_scalar(none[:, :], none[:, :], -1.0, float(2 * KTOP * TOK), ALU.is_equal, ALU.mult))
            def by4(a):
                return a.rearrange("p (r j) -> p r j", j=4)
            v.memset(rows[:, 0:2, 0, :], 0)
            v.memset(rows[:, MT // 4:, 1, :], 0)
            v.tensor_tensor(rows[:, 2:, 0, :], by4(slot[:, :]), by4(none[:, :]), ALU.add)
            link(v.tensor_copy(rows[:, 0:MT // 4, 1, :], by4(slot[:, :])))
            link(v.tensor_scalar(rows[:, 0:MT // 4, 1, :], rows[:, 0:MT // 4, 1, :], 1, None, ALU.arith_shift_right))

            def copy_row(r, h):
                v.tensor_copy(rows_c[h][:, :, :], rows[:, at(r), :, :].rearrange("p r a j -> p (r a) j")).then_inc(s_row, 1)
            copy_row(0, 0)
            copy_row(1, 1)

            link(v.tensor_tensor(tge[:, :, :], rf_iota[0:1, 0:MT].unsqueeze(2).to_broadcast([1, MT, E - 1]),
                                 tb[0:1, 1:E].unsqueeze(1).to_broadcast([1, MT, E - 1]), ALU.is_ge))
            link(v.tensor_reduce(tef[:, :], tge[:, :, :], AX.X, ALU.add))
            link(v.tensor_copy(tep[:, :], tef[:, 7::8]))
            for n in range(6, -1, -1):
                link(v.scalar_tensor_tensor(tep[:, :], tep[:, :], float(E), tef[:, n::8], ALU.mult, ALU.add))
            v.tensor_copy(te[:, :], tep[:, :]).then_inc(s_te, 1)

            def first_weights(i, j, e):
                need(dve, s_up, i - 1)
                v.tensor_copy(w1t[j % 2][:, :], w1s[:, bass.ds(e, 1), :].rearrange("p e f -> p (e f)")).then_inc(s_w1t, 1)

            dve.wait_ge(s_te, 1)
            dve.wait_ge(s_fw, 32)
            first = Experts(dve, 0)
            first.read()
            for j in range(3):
                first_weights(j, j, first(j))

            def step(i, j, left, expert):
                if j == 0 or j == 5 and left > 8:
                    expert.read()
                if left > 3:
                    first_weights(i + 3, j + 3, expert(j + 3))
                stored = 16 * (i // 8 + 1 if isinstance(i, int) else rounds[0] + 1)
                if j % 4 == 0:
                    dve.wait_ge(s_xtp, min(i + 4, MT) if isinstance(i, int) else i + 4)
                    for m in range(4):
                        dve.wait_ge(s_sc[j + m], stored)
                    copy_row(i // 4 + 2 if isinstance(i, int) else rounds[0] * 2 + 2 + j // 4, j // 4)
                e = expert(j)
                dve.wait_ge(s_dn, i + 3)
                dve.wait_ge(s_sc[j], stored)
                v.tensor_tensor(yb[j][:, :], PS[4 + j % 2][:, 0:D], b2s[:, bass.ds(e, 1), :].rearrange("p e f -> p (e f)"), ALU.add).then_inc(s_y, 1)
            tiles(dve, step, experts=True)

            dve.wait_ge(s_xr, 16 * (NT // SG))
            for q in range(NT // SG):
                dve.wait_ge(s_yr[q], 16)
                for b in range(SG):
                    t = q * SG + b
                    v.scalar_tensor_tensor(xres[q][:, b, :], yin[q][:, b, 0, :], gk[:, t:t + 1, 0], xres[q][:, b, :],
                                           ALU.mult, ALU.add).then_inc(s_o1, 1)
                dve.wait_ge(s_o1, (q + 1) * SG)
                dve.wait_ge(s_o2, q + 1)
                v.tensor_tensor(xres[q], xres[q], yin[q][:, :, 1, :], ALU.add).then_inc(s_o, 1)


def kernel(**inputs):
    import numpy as np
    import ml_dtypes
    import concourse.bacc as bacc
    from concourse.bass_utils import run_bass_kernel_spmd

    a = {k: np.asarray(v) for k, v in inputs.items()}
    c = {k[8:]: v for k, v in a.items() if k.startswith("L0_cond_")}
    f = {k[7:]: v for k, v in a.items() if k.startswith("L0_ffn_")}
    steps = a["fside_BxSxS_0"][:STEPS]
    wes = a["cond_2048"]
    cols = ([f["gate_w"].T, wes[:TYPES, :D].T, wes[:TYPES, D:].T, a["mask_BxS_ff0"][:STEPS].T]
            + [c[k].reshape(D, 1) for k in ("b_qin", "b_pl", "b_pc", "b_q", "b_k", "b_pk", "b_pv", "b_mu", "b_cb")]
            + [c["init_mem"].reshape(D, 1)]
            + [c["w_qin"].T] + [steps[t].T for t in range(STEPS)] + [c["w_pk"].T, c["w_pv"].T]
            + [c["w_k"], c["w_q"], c["w_pl"].T, c["w_pc"].T]
            + [c["w_v"][:, i * D:(i + 1) * D].T for i in range(3)]
            + [c["w_mu"][:, i * D:(i + 1) * D].T for i in range(2)]
            + [c["w_cb"][:, i * D:(i + 1) * D].T for i in range(2)]
            + [c["w_mu"][:, i * D:(i + 1) * D] for i in range(2)])
    sel_a = np.zeros((4, 32, UG, TYPES, N), np.float32)
    sel_c = np.zeros((4, 32, UG, TYPES, N), np.float32)
    for b in range(UG):
        for part in range(3):
            for r in range(TYPES):
                sel_a[b, part * AC + r, b, r, :] = 1
                sel_c[b, part * AC + TYPES + r, b, r, :] = 1
    eye = np.eye(128, dtype=np.float32)
    consts = np.concatenate([eye, -BIG * eye, sel_a.reshape(128, -1), sel_c.reshape(128, -1)], 1).astype(ml_dtypes.bfloat16)
    place = np.arange(128)
    rcf = np.concatenate([np.tile(place, (128, 1)), place[:, None],
                          np.tile(np.tril(np.ones((E, E)), -1).reshape(1, -1), (128, 1))], 1).astype(np.float32)
    cell = np.arange(NT * E)
    same = cell[:, None] % E == cell[None, :] % E
    earlier = same & (cell[:, None] // E < cell[None, :] // E)
    rcb = np.concatenate([place[:, None] < place[None, :]] + [earlier[h * 128:(h + 1) * 128] for h in range(2)]
                         + [same[h * 128:(h + 1) * 128, :E] for h in range(2)]
                         + [np.ones((128, 1)), np.tile(place, (128, 1)), np.tile(np.arange(NT * KTOP) + 1, (128, 1))],
                         1).astype(ml_dtypes.bfloat16)
    arrays = {
        "xT": a["x"].reshape(TOK, D).T, "x": a["x"], "mask": a["mask_BxS_ff1"].reshape(TOK), "adj": a["itok_BxSxS_0_4"],
        "fsT": a["fside_BxS_0"].T, "wpack": np.concatenate(cols, 1), "bvrow": c["b_v"],
        "w1": f["w1"].transpose(1, 0, 2), "b1": f["b1"].reshape(E * FC, 128).T,
        "w2": f["w2"].reshape(E, FC, 128, D).transpose(2, 0, 1, 3), "b2": f["b2"],
        "ident_d": np.concatenate([eye, np.tile(np.arange(E, 0, -1, dtype=np.float32), (128, 1))], 1), "bf_d": consts,
        "rcf_d": rcf, "rcb_d": rcb,
    }
    nc = bacc.Bacc("TRN2", target_bir_lowering=False, num_devices=1)
    args = {}
    for name, arr in list(arrays.items()):
        arrays[name] = arr = np.ascontiguousarray(arr)
        args[name] = nc.dram_tensor(name, arr.shape, mybir.dt.from_np(arr.dtype), kind="ExternalInput").ap()
    args["out"] = nc.dram_tensor("out", (B, N, D), mybir.dt.float32, kind="ExternalOutput").ap()
    build(nc, **args)
    return run_bass_kernel_spmd(nc, [arrays], core_ids=[0]).results[0]["out"]
```
